# Optimizing a Trainium2 kernel written in Bass

```python
import numpy as np
import jax
import jax.numpy as jnp

def _softmax(x, axis=-1):
    return jax.nn.softmax(x, axis=axis)

def _gelu(x):
    return jax.nn.gelu(x, approximate=True)

def _silu(x):
    return jax.nn.silu(x)

def _sigmoid(x):
    return jax.nn.sigmoid(x)

def _layernorm(x, axis=-1, eps=1e-05):
    m = jnp.mean(x, axis=axis, keepdims=True)
    v = jnp.var(x, axis=axis, keepdims=True)
    return (x - m) / jnp.sqrt(v + eps)

def _scatter_add(tgt, idx, src, axis=0):
    return tgt.at[idx].add(src)

def _segment_sum(src, seg, n):
    return jax.ops.segment_sum(src, seg, n)
kernel_name = 'mk_gnn_resnorm_d2_gnn_r8_2421aa'

def setup_inputs(seed: int=0):
    np.random.seed(seed)
    _w = jnp.asarray

    def _rec_inputs():
        import jax
        import jax.numpy as jnp
        _gk = jax.random.key(seed)
        x = -0.0003713 + 1 * jax.random.normal(jax.random.fold_in(_gk, 1), (6250, 256), jnp.float32)
        src = jax.random.randint(jax.random.fold_in(_gk, 2), (200000,), 0, 6250, jnp.int32)
        dst = jnp.minimum((6250 * jax.random.uniform(jax.random.fold_in(_gk, 3), (200000,)) ** 2.0).astype(jnp.int32), 49999)
        _o = jnp.argsort(dst, stable=True)
        src = src[_o]
        dst = dst[_o]
        edge_attr_128 = -5.16925e-05 + 1.00005 * jax.random.normal(jax.random.fold_in(_gk, 12), (200000, 128), jnp.float32)
        return (x, src, dst, edge_attr_128)
    x, src, dst, edge_attr_128 = _rec_inputs()

    def _L0_gnn_setup():
        import jax, jax.numpy as jnp
        import numpy as np
        N_NODES = 6250
        N_EDGES = 100000
        IN_DIM = 256
        OUT_DIM = 256
        EDGE_DIM = 128
        BN_EPS = 1e-05
        key = jax.random.key(seed)
        ks = jax.random.split(key, 10)
        s = lambda d: 1.0 / np.sqrt(d)
        return {'x': jax.random.normal(ks[0], (N_NODES, IN_DIM), dtype=jnp.float32), 'edge_index': jax.random.randint(ks[1], (2, N_EDGES), 0, N_NODES, dtype=jnp.int64), 'edge_attr': jax.random.normal(ks[2], (N_EDGES, EDGE_DIM), dtype=jnp.float32), 'W_edge': jax.random.uniform(ks[3], (EDGE_DIM, IN_DIM), jnp.float32, -s(EDGE_DIM), s(EDGE_DIM)), 'b_edge': jnp.zeros((IN_DIM,), jnp.float32), 'W1': jax.random.uniform(ks[4], (IN_DIM, OUT_DIM), jnp.float32, -s(IN_DIM), s(IN_DIM)), 'b1': jnp.zeros((OUT_DIM,), jnp.float32), 'W2': jax.random.uniform(ks[5], (OUT_DIM, OUT_DIM), jnp.float32, -s(OUT_DIM), s(OUT_DIM)), 'b2': jnp.zeros((OUT_DIM,), jnp.float32), 'eps': jnp.float32(0.0), 'gamma': jnp.ones((OUT_DIM,), jnp.float32), 'beta': jnp.zeros((OUT_DIM,), jnp.float32)}
    _L0_gnn_all = _L0_gnn_setup()
    _L0_gnn_in = {k: v for k, v in _L0_gnn_all.items() if k in ('W_edge', 'b_edge', 'W1', 'b1', 'W2', 'b2', 'eps', 'gamma', 'beta')}
    del _L0_gnn_all

    def _L1_gnn_setup():
        import jax, jax.numpy as jnp
        import numpy as np
        NEG = -1000.0
        SLOPE = 0.01
        N_NODES, N_EDGES, D_IN, D_OUT, N_HEADS = (12500, 200000, 256, 64, 4)
        key = jax.random.key(seed)
        k0, k1, k2, k3, k4 = jax.random.split(key, 5)
        h = jax.random.normal(k0, (N_NODES, D_IN), jnp.float32)
        src = jax.random.randint(k1, (N_EDGES,), 0, N_NODES)
        dst = jax.random.randint(k2, (N_EDGES,), 0, N_NODES)
        W = jax.random.normal(k3, (N_HEADS, D_IN, D_OUT), jnp.float32) / np.sqrt(D_IN)
        att = jax.random.normal(k4, (N_HEADS, 2 * D_OUT), jnp.float32) / np.sqrt(2.0 * D_OUT)
        return {'h': h, 'W': W, 'att': att, 'src': src, 'dst': dst}
    _L1_gnn_all = _L1_gnn_setup()
    _L1_gnn_in = {k: v for k, v in _L1_gnn_all.items() if k in ('W', 'att')}
    del _L1_gnn_all
    return {'x': x, 'src': src, 'dst': dst, 'edge_attr_128': edge_attr_128, 'L0_gnn_W_edge': _L0_gnn_in['W_edge'], 'L0_gnn_b_edge': _L0_gnn_in['b_edge'], 'L0_gnn_W1': _L0_gnn_in['W1'], 'L0_gnn_b1': _L0_gnn_in['b1'], 'L0_gnn_W2': _L0_gnn_in['W2'], 'L0_gnn_b2': _L0_gnn_in['b2'], 'L0_gnn_eps': _L0_gnn_in['eps'], 'L0_gnn_gamma': _L0_gnn_in['gamma'], 'L0_gnn_beta': _L0_gnn_in['beta'], 'L1_gnn_W': _L1_gnn_in['W'], 'L1_gnn_att': _L1_gnn_in['att']}

def reference(x, src, dst, edge_attr_128, L0_gnn_W_edge, L0_gnn_b_edge, L0_gnn_W1, L0_gnn_b1, L0_gnn_W2, L0_gnn_b2, L0_gnn_eps, L0_gnn_gamma, L0_gnn_beta, L1_gnn_W, L1_gnn_att):
    import jax
    import jax.numpy as jnp

    def _L0_gnn_ref(x, edge_index, edge_attr, W_edge, b_edge, W1, b1, W2, b2, eps, gamma, beta):
        import jax, jax.numpy as jnp
        import numpy as np
        N_NODES = 6250
        N_EDGES = 100000
        IN_DIM = 256
        OUT_DIM = 256
        EDGE_DIM = 128
        BN_EPS = 1e-05
        src, dst = (edge_index[0], edge_index[1])
        e = edge_attr @ W_edge + b_edge
        msg = jax.nn.relu(x[src] + e)
        agg = jax.ops.segment_sum(msg, dst, num_segments=x.shape[0])
        h = (1.0 + eps) * x + agg
        h = jax.nn.relu(h @ W1 + b1) @ W2 + b2
        mean = jnp.mean(h, axis=0)
        var = jnp.var(h, axis=0)
        h = (h - mean) * jax.lax.rsqrt(var + BN_EPS) * gamma + beta
        return jax.nn.relu(h)

    def _L1_gnn_ref(h, W, att, src, dst):
        import jax, jax.numpy as jnp
        import numpy as np
        NEG = -1000.0
        SLOPE = 0.01
        N_NODES, N_EDGES, D_IN, D_OUT, N_HEADS = (12500, 200000, 256, 64, 4)
        N = h.shape[0]
        H, _, F = W.shape
        z = jnp.einsum('nd,hdf->nhf', h, W)
        a_src, a_dst = (att[:, :F], att[:, F:])
        es = jnp.einsum('nhf,hf->nh', z, a_src)
        ed = jnp.einsum('nhf,hf->nh', z, a_dst)
        e = jax.nn.leaky_relu(es[src] + ed[dst], SLOPE)
        e = jnp.where(e == 0.0, NEG, e)
        m = jax.ops.segment_max(e, dst, num_segments=N)
        m = jnp.where(jnp.isfinite(m), m, 0.0)
        ex = jnp.exp(e - m[dst])
        denom = jax.ops.segment_sum(ex, dst, num_segments=N)
        safe = jnp.where(denom[dst] > 0.0, denom[dst], 1.0)
        alpha = ex / safe
        out = jax.ops.segment_sum(alpha[:, :, None] * z[src], dst, num_segments=N)
        return out.reshape(N, H * F)
    edge_index = jnp.stack([src, dst])
    x = _layernorm(x + _L0_gnn_ref(x, edge_index, edge_attr_128, L0_gnn_W_edge, L0_gnn_b_edge, L0_gnn_W1, L0_gnn_b1, L0_gnn_W2, L0_gnn_b2, L0_gnn_eps, L0_gnn_gamma, L0_gnn_beta), axis=-1)
    x = _layernorm(x + _L1_gnn_ref(x, L1_gnn_W, L1_gnn_att, src, dst), axis=-1)
    return x

_drawn_inputs = setup_inputs


def setup_inputs(seed=0):
    import zlib

    import numpy as np

    out = dict(_drawn_inputs(seed))
    spreads = {'L0_gnn_b_edge': (0.0, 0.1),
     'L0_gnn_b1': (0.0, 0.8),
     'L0_gnn_b2': (0.0, 0.8),
     'L0_gnn_gamma': (1.0, 0.2),
     'L0_gnn_beta': (0.0, 0.1)}
    factors = {}
    for name, (base, spread) in spreads.items():
        noise = np.random.default_rng([zlib.crc32(name.encode()), seed]).standard_normal(out[name].shape)
        drawn = base * np.exp(spread * noise) if base else spread * noise
        out[name] = jnp.asarray(drawn.astype(out[name].dtype))
    for name, factor in factors.items():
        out[name] = (out[name] * factor).astype(out[name].dtype)
    return out
```

```python
from contextlib import ExitStack

import concourse.bass as bass
from concourse import mybir

ALU = mybir.AluOpType
ACT = mybir.ActivationFunctionType
AX = mybir.AxisListType
F32 = mybir.dt.float32
BF16 = mybir.dt.bfloat16
I32 = mybir.dt.int32

P = 128
NODES = 6250
EDGES = 200000
D = 256
HALF = D // P
EDGE_D = 128
HEADS = 4
HEAD_D = D // HEADS
J = 8
GROUP = P * J
GROUPS = -(-EDGES // GROUP)
EPAD = GROUPS * GROUP
RING = 4
ROUNDS = GROUPS // RING
PAIRS = J // 2
WIN = 64
ROW = D + HEADS
CHUNK = 448
CHUNKS = -(-NODES // CHUNK)
NPAD = CHUNK * CHUNKS
TAIL = NODES - CHUNK * (CHUNKS - 1)
SUB = CHUNK // 4
ACC_W = NPAD + WIN
LINE = EPAD // P
BN_EPS = 1e-5
LN_EPS = 1e-5
SLOPE = 0.01
NEG = -1000.0
FAR = -1e30
FLOOR = -80.0


def build(nc, t):
    with ExitStack() as ctx:
        def sb(name, shape, dt=F32):
            return ctx.enter_context(nc.sbuf_tensor(name, shape, dt))

        def sem(name):
            return ctx.enter_context(nc.semaphore(name))

        def dram(name, shape, dt=F32):
            return nc.dram_tensor(name, shape, dt).ap()

        z_tab = dram("z_tab", (NPAD, ROW))
        es_tab = dram("es_tab", (NPAD, HEADS))
        ed_tab = dram("ed_tab", (NPAD, HEADS))
        score_tab = dram("score_tab", (GROUPS, P, J * HEADS))
        expo_tab = dram("expo_tab", (GROUPS, P, J * HEADS))

        acc = sb("acc", [P, HALF, ACC_W])
        node_x = sb("node_x", [P, HALF, NPAD])
        rows = sb("rows", [P, RING, J, ROW])
        edge_in = sb("edge_in", [P, RING, GROUP])
        den = sb("den", [HEADS, ACC_W])
        onehot = sb("onehot", [P, 2, J, WIN])
        idx = sb("idx", [P, RING, J], I32)
        dst_off = sb("dst_off", [P, GROUPS, J])
        off_here = sb("off_here", [P, J])
        firsts = sb("firsts", [P, 2, GROUPS], I32)
        first_f = sb("first_f", [P, GROUPS])
        plan_f = sb("plan_f", [1, 3, GROUPS])
        plan = sb("plan", [1, 3, GROUPS], I32)
        agg_sb = sb("agg_sb", [WIN, ROW])
        expo = sb("expo", [P, RING, J * HEADS])
        iota_i = sb("iota_i", [P, WIN], I32)
        iota = sb("iota", [P, WIN])
        ident = sb("ident", [P, P])
        mean_w = sb("mean_w", [P, P])
        ones_b = sb("ones_b", [3, P], BF16)
        w_edge = sb("w_edge", [P, D])
        b_three = sb("b_three", [3, D], BF16)
        w1 = sb("w1", [P, HALF, D])
        w2 = sb("w2", [P, HALF, D])
        wz = sb("wz", [P, HALF, D + 2 * HEADS])
        cols = sb("cols", [P, 4, HALF])
        eps1 = sb("eps1", [P, 1])
        ln_eps = sb("ln_eps", [P, 1])
        bn_eps = sb("bn_eps", [P, 1])
        stats = sb("stats", [P, HALF, CHUNKS, 6])
        mv = sb("mv", [P, HALF, 2])
        bn_scale = sb("bn_scale", [P, HALF])
        bn_shift = sb("bn_shift", [P, HALF])
        bn_tmp = sb("bn_tmp", [P, HALF])
        head_sel = sb("head_sel", [HEADS, HALF, P])

        early = node_x[:, :, :].rearrange("p k n -> p (k n)")
        b_row = early[0:1, 0:D]
        b_rest = early[0:1, 2 * D:4 * D].rearrange("p (a n) -> p a n", a=2)
        b_part = early[0:1, 4 * D:4 * D + 3 * D // 2].bitcast(BF16).rearrange("p (a n) -> p a n", a=3)
        att = early[:, 10 * D:12 * D].rearrange("p (a n) -> p a n", a=2)

        dst_raw = early[:, 12 * D:12 * D + GROUPS * J].bitcast(I32)

        spare = rows[:, :, :, :].rearrange("p r j c -> p (r j c)")

        def piece(n, width=HALF * CHUNK):
            return spare[:, n * HALF * CHUNK:n * HALF * CHUNK + width]

        def halves(ap):
            return ap.rearrange("p (k n) -> p k n", k=HALF)

        buf_a, buf_b, buf_c, buf_d = (halves(piece(n)) for n in range(4))
        z_sb = piece(4, 4 * (D + 2 * HEADS)).rearrange("p (s c) -> p s c", s=4)
        rstd = piece(6, CHUNK)
        fin = piece(4, 4 * D).rearrange("p (s c) -> p s c", s=4)
        after_rstd = spare[:, 6 * HALF * CHUNK + CHUNK:]
        fin_stats = after_rstd[:, 0:24].rearrange("p (s c) -> p s c", s=4)
        fin_mv = after_rstd[:, 24:32].rearrange("p (s c) -> p s c", s=4)
        fin_r, fin_s = after_rstd[:, 32:36], after_rstd[:, 36:40]

        flat = acc[:, :, :].rearrange("p k n -> p (k n)")

        def acc_line(n):
            return flat[:, n * LINE * HEADS:(n + 1) * LINE * HEADS]

        def line_dst(n):
            return spare[:, n * LINE:(n + 1) * LINE].bitcast(I32)

        pen_in, pen_out = (spare[:, n * LINE:(n + 1) * LINE] for n in (3, 4))
        edge_flat = edge_in[:, :, :].rearrange("p r n -> p (r n)")
        run_max = edge_flat[:, 0:LINE]
        lasts = edge_flat[:, LINE:LINE + 16]
        carry_t = edge_flat[:, LINE + 16:LINE + 16 + 2 * P + 2]
        carry = edge_flat[:, LINE + 300:LINE + 300 + 2 * HEADS]
        carry_sb = edge_flat[:, LINE + 320:LINE + 320 + 2 * P]

        def score_rows(n):
            return spare[:, n * J * HEADS:(n + 1) * J * HEADS]

        banks = [ctx.enter_context(nc.psum_tensor(f"bank{n}", [P, 512], F32)) for n in range(8)]
        agg_ps, turn_ps = banks[4], banks[5]

        const_in = sem("const_in")
        dst_in = sem("dst_in")
        passed = sem("passed")
        consts = sem("consts")
        acc_zeroed = sem("acc_zeroed")
        planned = sem("planned")
        b_split = sem("b_split")
        b_in = sem("b_in")

        class Layer:
            def __init__(self, n):
                s = lambda name: sem(f"{name}{n}")
                self.idx_in = [s(f"idx_in_{u}_") for u in range(RING)]
                self.rows_in = [s(f"rows_in_{u}_") for u in range(RING)]
                self.edge_in = [s(f"edge_in_{u}_") for u in range(RING)]
                self.edge_done, self.summed, self.msg_ready = s("edge_done"), s("summed"), s("msg_ready")
                self.onehot_ready, self.agg_ready, self.agg_copied = s("onehot"), s("agg"), s("aggc")
                self.turned, self.group_done = s("turned"), s("group_done")
                self.x_onehot, self.x_agg, self.x_copied = s("x_onehot"), s("x_agg"), s("x_copied")
                self.x_turned, self.x_added = s("x_turned"), s("x_added")
                self.acc_zero = s("acc_zero")

        layer0, layer1 = Layer(0), Layer(1)

        chunk_x = sem("chunk_x")
        a_hid, a_pe1, a_act1, a_pe2, a_act2, a_stat = (sem(f"a_{x}") for x in ("h", "p1", "r1", "p2", "r2", "st"))
        bn_ready = sem("bn_ready")
        bn_sqrt = sem("bn_sqrt")
        bn_var = sem("bn_var")
        chunk_y = sem("chunk_y")
        l_bn, l_res, l_mean, l_cen, l_sq, l_var, l_std, l_x, l_z, l_zc, l_out = (
            sem(f"l_{x}") for x in ("bn", "res", "mean", "cen", "sq", "var", "std", "x", "z", "zc", "out"))
        wz_ready = sem("wz_ready")
        att_ready = sem("att_ready")
        s_idx = [sem(f"s_idx{u}") for u in range(2)]
        s_rows = [sem(f"s_rows{u}") for u in range(2)]
        s_score = sem("s_score")
        s_stored = [sem(f"s_stored{u}") for u in range(2)]
        m_in = sem("m_in")
        m_pen = sem("m_pen")
        m_last, m_lastT, m_carry, m_carryT = (sem(f"m_{x}") for x in ("last", "lastT", "carry", "carryT"))
        m_done = sem("m_done")
        m_out = sem("m_out")
        f_rden, f_spread, f_sum, f_turn, f_mv, f_std, f_r, f_nrm, f_out = (
            sem(f"f_{x}") for x in ("rden", "spread", "sum", "turn", "mv", "std", "r", "nrm", "out"))

        block = ctx.enter_context(nc.Block())


        def rounds(eng, body, tail=None):
            for u in range(RING):
                body(0, u, u)
            with eng.Fori(1, ROUNDS) as i:
                for u in range(RING):
                    body(i, u, i * RING + u)

        def first_round(i):
            return isinstance(i, int)

        def pass_loads(sp, L, layer):
            def body(i, u, g):
                if not first_round(i):
                    sp.wait_ge(L.rows_in[u], 16 * J * i)
                sp.dma_start(idx[:, u, :], t["src_idx"][g]).then_inc(L.idx_in[u], 16)
                if layer == 0:
                    if not first_round(i):
                        sp.wait_ge(L.edge_done, PAIRS * (g - RING + 1))
                    sp.dma_start(edge_in[:, u, :], t["edge_t"][g]).then_inc(L.edge_in[u], 16)
                else:
                    if not first_round(i):
                        sp.wait_ge(L.group_done, g - RING + 1)
                    sp.dma_start(expo[:, u, :], expo_tab[g]).then_inc(L.edge_in[u], 16)
            rounds(sp, body)

        def pass_gathers(pool, L, layer):
            table, width = (t["x"], D) if layer == 0 else (z_tab, ROW)

            def body(i, u, g):
                if not first_round(i):
                    pool.wait_ge(L.group_done, g - RING + 1)
                    pool.sem_inc(passed, 1)
                pool.wait_ge(L.idx_in[u], 16 * i + 16)
                if not first_round(i):
                    pool.sem_inc(passed, 1)
                for j in range(J):
                    nc.gpsimd.indirect_dma_start(
                        rows[:, u, j, 0:width], None, table,
                        bass.IndirectOffsetOnAxis(ap=idx[:, u, j:j + 1], axis=0)).then_inc(L.rows_in[u], 16)
            rounds(pool, body)

        def turn(pe, L, dst_sem):
            pe.sem_inc(passed, 1)
            for k in range(HALF):
                last = pe.transpose(turn_ps[:, k * WIN:(k + 1) * WIN], agg_sb[:, k * P:(k + 1) * P],
                                    ident[0:WIN, 0:WIN])
            if L is layer1:
                last = pe.transpose(turn_ps[0:HEADS, HALF * WIN:(HALF + 1) * WIN], agg_sb[:, D:ROW],
                                    ident[0:WIN, 0:WIN])
            last.then_inc(dst_sem, 1)

        def pass_matmuls(pe, L, layer):
            width = D if layer == 0 else ROW

            def edge_products(i, u, g, pairs):
                for q in pairs:
                    if q == 0:
                        pe.wait_ge(L.edge_in[u], 16 * i + 16)
                    if not (first_round(i) and g == 0):
                        pe.wait_ge(L.summed, PAIRS * (g - 1) + q + 1)
                    for h in range(2):
                        j = 2 * q + h
                        out = banks[q][:, h * D:(h + 1) * D]
                        pe.matmul(out, ones_b[:, :], b_three[:, :], start=True, stop=False)
                        last = pe.matmul(out, edge_in[:, u, j * P:(j + 1) * P], w_edge[:, :], start=False, stop=True)
                    last.then_inc(L.edge_done, 1)

            def sum_window(u, g, dst_sem):
                for j in range(J):
                    last = pe.matmul(agg_ps[0:WIN, 0:width], onehot[:, u % 2, j, :], rows[:, u, j, 0:width],
                                     start=(j == 0), stop=(j == J - 1))
                last.then_inc(dst_sem, 1)

            def sum_first(u, g):
                pe.wait_ge(L.onehot_ready, g + 1)
                pe.wait_ge(L.msg_ready, (PAIRS if layer == 0 else 2) * (g + 1))
                sum_window(u, g, L.agg_ready)

            def finish(u, g, at_start):
                pe.wait_ge(L.agg_copied, g + 1)
                if not at_start:
                    pe.wait_ge(L.group_done, g)
                turn(pe, L, L.turned)
                windows = pe.value_load(plan[0:1, 1, bass.ds(g, 1)], min_val=1, max_val=CHUNKS * 8)
                before = pe.value_load(plan[0:1, 2, bass.ds(g, 1)], min_val=0, max_val=1 << 20)
                with pe.If(windows > 1):
                    with pe.Fori(1, windows) as k:
                        pe.wait_ge(L.x_onehot, before + k)
                        sum_window(u, g, L.x_agg)
                        pe.wait_ge(L.x_copied, before + k)
                        turn(pe, L, L.x_turned)

            def body(i, u, g):
                start = first_round(i) and g == 0
                if layer == 0:
                    edge_products(i, u, g, range(PAIRS - 1))
                if not start:
                    sum_first((u - 1) % RING, g - 1)
                if layer == 0:
                    edge_products(i, u, g, range(PAIRS - 1, PAIRS))
                if not start:
                    finish((u - 1) % RING, g - 1, first_round(i) and g == 1)
            rounds(pe, body)
            sum_first(RING - 1, GROUPS - 1)
            finish(RING - 1, GROUPS - 1, False)

        def pass_act(act, L, layer):
            width = D if layer == 0 else ROW

            def copy_window(dst_sem):
                act.copy(agg_sb[:, 0:width], agg_ps[0:WIN, 0:width]).then_inc(dst_sem, 1)

            def copy_first(g, at_start):
                act.wait_ge(L.agg_ready, g + 1)
                if not at_start:
                    act.wait_ge(L.group_done, g)
                copy_window(L.agg_copied)

            def extras(g):
                windows = act.value_load(plan[0:1, 1, bass.ds(g, 1)], min_val=1, max_val=CHUNKS * 8)
                before = act.value_load(plan[0:1, 2, bass.ds(g, 1)], min_val=0, max_val=1 << 20)
                with act.If(windows > 1):
                    with act.Fori(1, windows) as k:
                        act.wait_ge(L.x_agg, before + k)
                        copy_window(L.x_copied)

            def body(i, u, g):
                start = first_round(i) and g == 0
                if layer == 0:
                    for q in range(PAIRS):
                        act.wait_ge(L.summed, PAIRS * g + q + 1)
                        pair = rows[:, u, 2 * q:2 * q + 2, 0:D]
                        if q == PAIRS - 1 and not start:
                            copy_first(g - 1, first_round(i) and g == 1)
                        act.activation(pair, pair, ACT.Relu).then_inc(L.msg_ready, 1)
                else:
                    act.wait_ge(L.edge_in[u], 16 * i + 16)
                    act.wait_ge(L.rows_in[u], 16 * J * (i + 1))
                    act.activation(rows[:, u, :, D:ROW], expo[:, u, :].rearrange("p (j h) -> p j h", j=J),
                                   ACT.Exp).then_inc(L.summed, 1)
                    if not start:
                        copy_first(g - 1, first_round(i) and g == 1)
                if not start:
                    extras(g - 1)
            rounds(act, body)
            copy_first(GROUPS - 1, False)
            extras(GROUPS - 1)

        def pass_vector(dve, L, layer):
            window_base = dve.alloc_register(f"window_base{layer}")

            def add_window(base):
                at = bass.ds(base, WIN)
                last = dve.tensor_tensor(acc[:, :, at], acc[:, :, at],
                                         turn_ps[:, 0:HALF * WIN].rearrange("p (k n) -> p k n", k=HALF), ALU.add)
                if layer == 1:
                    last = dve.tensor_tensor(den[:, at], den[:, at],
                                             turn_ps[0:HEADS, HALF * WIN:(HALF + 1) * WIN], ALU.add)
                return last

            def finish(u, g):
                base = dve.value_load(plan[0:1, 0, bass.ds(g, 1)], min_val=0, max_val=NODES)
                windows = dve.value_load(plan[0:1, 1, bass.ds(g, 1)], min_val=1, max_val=CHUNKS * 8)
                before = dve.value_load(plan[0:1, 2, bass.ds(g, 1)], min_val=0, max_val=1 << 20)
                dve.wait_ge(L.turned, g + 1)
                add_window(base)
                with dve.If(windows > 1):
                    dve.tensor_copy(off_here[:, :], offsets(g))
                    with dve.Fori(1, windows) as k:
                        dve.drain()
                        dve.tensor_scalar(off_here[:, :], off_here[:, :], float(WIN), None, ALU.subtract)
                        dve.drain()
                        make_onehot(u, off_here[:, :], L.x_onehot)
                        dve.wait_ge(L.x_turned, before + k)
                        dve.reg_mov(window_base, base + k * WIN)
                        add_window(dve.snap(window_base, min_val=0, max_val=NODES))
                dve.drain().then_inc(L.group_done, 1)

            def offsets(g):
                return dst_off[:, bass.ds(g, 1), :].rearrange("p g j -> p (g j)")

            def make_onehot(u, off, dst_sem):
                dve.tensor_tensor(onehot[:, u % 2, :, :], off.unsqueeze(2).to_broadcast([P, J, WIN]),
                                  iota[:, :].unsqueeze(1).to_broadcast([P, J, WIN]), ALU.is_equal).then_inc(dst_sem, 1)

            def body(i, u, g):
                make_onehot(u, offsets(g), L.onehot_ready)
                if layer == 0:
                    dve.wait_ge(L.rows_in[u], 16 * J * (i + 1))
                    for q in range(PAIRS):
                        dve.wait_ge(L.edge_done, PAIRS * g + q + 1)
                        pair = rows[:, u, 2 * q:2 * q + 2, 0:D]
                        dve.tensor_tensor(pair, pair, banks[q][:, :].rearrange("p (j d) -> p j d", j=2),
                                          ALU.add).then_inc(L.summed, 1)
                else:
                    dve.wait_ge(L.summed, g + 1)
                    for q in range(2):
                        js = slice(q * J // 2, (q + 1) * J // 2)
                        z = rows[:, u, js, 0:D].rearrange("p j (h f) -> p j h f", h=HEADS)
                        w = rows[:, u, js, D:ROW].unsqueeze(3).to_broadcast([P, J // 2, HEADS, HEAD_D])
                        dve.tensor_tensor(z, z, w, ALU.mult).then_inc(L.msg_ready, 1)
                if not (first_round(i) and g == 0):
                    finish((u - 1) % RING, g - 1)
            rounds(dve, body)
            finish(RING - 1, GROUPS - 1)

        @block.sync
        def _(sp):
            for out, of in ((w_edge[:, :], t["w_edge"]), (b_row, t["b_edge"]),
                            (eps1[:, :], t["eps"].to_broadcast([P, 1])),
                            (cols[:, 0, :], t["b1"]), (cols[:, 1, :], t["b2"]),
                            (cols[:, 2, :], t["gamma"]), (cols[:, 3, :], t["beta"]),
                            (w1[:, :, :], t["w1"]), (w2[:, :, :], t["w2"]), (wz[:, :, 0:D], t["wz"]),
                            (att[:, 0, :], t["att_src"].to_broadcast([P, D])),
                            (att[:, 1, :], t["att_dst"].to_broadcast([P, D])),):
                sp.dma_start(out, of).then_inc(const_in, 16)
            sp.dma_start(firsts[:, 0, :], t["first"].to_broadcast([P, GROUPS])).then_inc(dst_in, 16)
            sp.dma_start(firsts[:, 1, :], t["last"].to_broadcast([P, GROUPS])).then_inc(dst_in, 16)
            sp.dma_start(dst_raw[:, :], t["dst_pm"]).then_inc(dst_in, 16)
            sp.wait_ge(b_split, 1)
            for n in range(3):
                sp.dma_start(b_three[n:n + 1, :], b_part[:, n, :]).then_inc(b_in, 16)
            pass_loads(sp, layer0, 0)

            sp.wait_ge(layer0.group_done, GROUPS)
            with sp.Fori(0, CHUNKS) as c:
                sp.wait_ge(a_hid, c)
                sp.dma_start(buf_a, t["x_t"][:, :, bass.ds(c * CHUNK, CHUNK)]).then_inc(chunk_x, 16)
            sp.wait_ge(a_hid, CHUNKS)
            with sp.Fori(0, CHUNKS) as c:
                sp.wait_ge(l_res, c)
                sp.dma_start(buf_a, t["x_t"][:, :, bass.ds(c * CHUNK, CHUNK)]).then_inc(chunk_y, 16)
                sp.wait_ge(l_zc, c * 4 + 4)
                at = bass.ds(c * CHUNK, CHUNK)
                for tab, lo, hi in ((z_tab, 0, ROW), (es_tab, D, D + HEADS), (ed_tab, D + HEADS, D + 2 * HEADS)):
                    sp.dma_start(tab[at, :].rearrange("(s p) c -> p s c", s=4), z_sb[0:SUB, :, lo:hi]).then_inc(l_out, 16)
            sp.wait_ge(l_out, 48 * CHUNKS)

            with sp.Fori(0, GROUPS // 2) as i:
                for u in range(2):
                    g = i * 2 + u
                    sp.wait_ge(s_rows[u], 2 * 16 * J * i)
                    sp.dma_start(idx[:, u, :], t["src_idx"][g]).then_inc(s_idx[u], 16)
                    sp.dma_start(idx[:, 2 + u, :], t["dst_idx"][g]).then_inc(s_idx[u], 16)
                for u in range(2):
                    g = i * 2 + u
                    sp.wait_ge(s_score, g + 1)
                    sp.dma_start(score_tab[g], expo[:, u, :]).then_inc(s_stored[u], 16)
            for u in range(2):
                sp.wait_ge(s_stored[u], 16 * (GROUPS // 2))
            line = score_tab.rearrange("g p c -> (g p c)").rearrange("(q n) -> q n", q=P)
            sp.dma_start(acc_line(0), line).then_inc(m_in, 16)
            for n in range(3):
                sp.dma_start(line_dst(n), t["dst_ext"][:, n:n + EPAD].rearrange("a (q n) -> (a q) n", q=P)).then_inc(m_in, 16)
            sp.wait_ge(m_done, 1)
            oline = expo_tab.rearrange("g p c -> (g p c)").rearrange("(q n) -> q n", q=P)
            sp.dma_start(oline, acc_line(0)).then_inc(m_out, 16)
            sp.wait_ge(m_out, 16)
            pass_loads(sp, layer1, 1)

            def store(c, at, n):
                sp.wait_ge(f_nrm, c * 4 + 4)
                whole = n // SUB
                sp.dma_start(t["out"][bass.ds(c * CHUNK, whole * SUB), :]
                             .rearrange("(s p) c -> p s c", s=whole), fin[0:SUB, 0:whole, :]).then_inc(f_out, 16)
                if n > whole * SUB:
                    rest = n - whole * SUB
                    sp.dma_start(t["out"][c * CHUNK + whole * SUB:c * CHUNK + n, :], fin[0:rest, whole, :]).then_inc(f_out, 16)

            with sp.Fori(0, CHUNKS - 1) as c:
                store(c, None, CHUNK)
            store(CHUNKS - 1, None, TAIL)
            sp.wait_ge(f_out, 16 * (CHUNKS + 1))

        @block.gpsimd
        def _(pool):
            nc.gpsimd.iota(iota_i[:, :], pattern=[[1, WIN]], base=0, channel_multiplier=0).then_inc(consts, 1)
            nc.gpsimd.memset(ident[:, :], 0.0)
            nc.gpsimd.memset(head_sel[:, :, :], 1.0)
            pool.drain()
            nc.gpsimd.affine_select(out=ident[:, :], in_=ident[:, :], compare_op=ALU.not_equal, fill=1.0, base=0,
                                    pattern=[[-1, P]], channel_multiplier=1)
            sel = head_sel[:, :, :]
            nc.gpsimd.affine_select(out=sel, in_=sel, compare_op=ALU.is_ge, fill=0.0, base=0,
                                    pattern=[[P, HALF], [1, P]], channel_multiplier=-HEAD_D)
            pool.drain()
            nc.gpsimd.affine_select(out=sel, in_=sel, compare_op=ALU.is_ge, fill=0.0, base=HEAD_D - 1,
                                    pattern=[[-P, HALF], [-1, P]], channel_multiplier=HEAD_D)
            pool.drain().then_inc(consts, 1)
            pass_gathers(pool, layer0, 0)

            pool.wait_ge(l_out, 48 * CHUNKS)
            with pool.Fori(0, GROUPS // 2) as i:
                for u in range(2):
                    g = i * 2 + u
                    pool.wait_ge(s_score, g - 1) if False else None
                    pool.wait_ge(s_idx[u], 32 * i + 32)
                    pool.sem_inc(passed, 1)
                    for j in range(J):
                        for n, tab in ((u, es_tab), (2 + u, ed_tab)):
                            nc.gpsimd.indirect_dma_start(
                                score_rows(n)[:, j * HEADS:(j + 1) * HEADS], None, tab,
                                bass.IndirectOffsetOnAxis(ap=idx[:, n, j:j + 1], axis=0)).then_inc(s_rows[u], 16)
            pool.wait_ge(m_out, 16)
            nc.gpsimd.memset(acc[:, :, :], 0.0)
            nc.gpsimd.memset(den[:, :], 0.0)
            pool.drain().then_inc(layer1.acc_zero, 1)
            pass_gathers(pool, layer1, 1)

        @block.tensor
        def _(pe):
            pe.wait_ge(const_in, 16 * 12)
            pe.wait_ge(b_in, 48)
            pe.wait_ge(consts, 2)
            pe.wait_ge(acc_zeroed, 1)
            pe.wait_ge(planned, 1)
            pass_matmuls(pe, layer0, 0)

            def product(w, x, ready, out, done):
                for m in range(HALF):
                    for k in range(HALF):
                        last = pe.matmul(banks[out + m][:, 0:CHUNK], w[:, k, m * P:(m + 1) * P], x[:, k, :],
                                         start=(k == 0), stop=(k == HALF - 1))
                last.then_inc(done, 1)

            pe.wait_ge(layer0.group_done, GROUPS)
            with pe.Fori(0, CHUNKS) as c:
                pe.wait_ge(a_hid, c + 1)
                product(w1, buf_b, None, 0, a_pe1)
                pe.wait_ge(a_act1, c + 1)
                product(w2, buf_c, None, 2, a_pe2)
            pe.wait_ge(wz_ready, 1)
            pe.wait_ge(a_act2, CHUNKS)
            with pe.Fori(0, CHUNKS) as c:
                pe.wait_ge(l_res, c + 1)
                for k in range(HALF):
                    last = pe.matmul(banks[0][:, 0:CHUNK], mean_w[:, :], buf_b[:, k, :], start=(k == 0), stop=(k == 1))
                last.then_inc(l_mean, 1)
                pe.wait_ge(l_sq, c + 1)
                for k in range(HALF):
                    last = pe.matmul(banks[1][:, 0:CHUNK], mean_w[:, :], buf_d[:, k, :], start=(k == 0), stop=(k == 1))
                last.then_inc(l_var, 1)
                pe.wait_ge(l_x, c + 1)
                for s in range(4):
                    pe.wait_ge(l_zc, 4 * c + s - 3) if False else None
                    for k in range(HALF):
                        last = pe.matmul(banks[2 + s][0:SUB, 0:D + 2 * HEADS], buf_d[:, k, s * SUB:(s + 1) * SUB],
                                         wz[:, k, :], start=(k == 0), stop=(k == 1))
                    last.then_inc(l_z, 1)

            for n in range(2):
                pe.wait_ge(m_last, n + 1)
                pe.transpose(banks[0][0:HEADS, 0:P], lasts[:, 0:HEADS], ident[:, :])
                pe.transpose(banks[0][0:HEADS, P:2 * P], lasts[:, HEADS:2 * HEADS], ident[:, :]).then_inc(m_lastT, 1)
                pe.wait_ge(m_carry, n + 1)
                pe.transpose(banks[1][:, 0:HEADS], carry_t[0:HEADS, n:n + P], ident[0:HEADS, 0:HEADS]).then_inc(m_carryT, 1)
            pe.wait_ge(layer1.acc_zero, 1)
            pass_matmuls(pe, layer1, 1)
            pe.wait_ge(layer1.group_done, GROUPS)
            with pe.Fori(0, CHUNKS) as c:
                pe.wait_ge(f_rden, c + 1)
                for k in range(HALF):
                    last = pe.matmul(banks[k][:, 0:CHUNK], head_sel[:, k, :], rstd[0:HEADS, :], start=True, stop=True)
                last.then_inc(f_spread, 1)
                pe.wait_ge(f_sum, c + 1)
                for s in range(4):
                    for k in range(HALF):
                        last = pe.transpose(banks[2 + s][0:SUB, k * P:(k + 1) * P], buf_b[:, k, s * SUB:(s + 1) * SUB],
                                            ident[:, :])
                    last.then_inc(f_turn, 1)


        @block.scalar
        def _(act):
            act.wait_ge(planned, 1)
            pass_act(act, layer0, 0)
            with act.Fori(0, CHUNKS) as c:
                act.wait_ge(a_pe1, c + 1)
                for k in range(HALF):
                    last = act.activation(buf_c[:, k, :], banks[k][:, 0:CHUNK], ACT.Relu, bias=cols[:, 0, k:k + 1])
                last.then_inc(a_act1, 1)
                act.wait_ge(a_pe2, c + 1)
                for k in range(HALF):
                    last = act.activation(node_x[:, k, bass.ds(c * CHUNK, CHUNK)], banks[2 + k][:, 0:CHUNK],
                                          ACT.Identity, bias=cols[:, 1, k:k + 1])
                last.then_inc(a_act2, 1)
            act.wait_ge(bn_var, 1)
            act.activation(bn_tmp[:, :], mv[:, :, 1], ACT.Sqrt, bias=bn_eps[:, :]).then_inc(bn_sqrt, 1)
            act.wait_ge(bn_ready, 1)
            with act.Fori(0, CHUNKS) as c:
                at = bass.ds(c * CHUNK, CHUNK)
                act.wait_ge(l_x, c)
                for k in range(HALF):
                    last = act.activation(buf_c[:, k, :], node_x[:, k, at], ACT.Relu,
                                          bias=bn_shift[:, k:k + 1], scale=bn_scale[:, k:k + 1])
                last.then_inc(l_bn, 1)
                act.wait_ge(l_cen, c + 1)
                act.wait_ge(l_zc, 4 * c)
                act.activation(buf_d, buf_c, ACT.Square).then_inc(l_sq, 1)
                act.wait_ge(l_var, c + 1)
                act.activation(rstd, banks[1][:, 0:CHUNK], ACT.Sqrt, bias=ln_eps[:, :]).then_inc(l_std, 1)
                act.wait_ge(l_out, 48 * c)
                for s in range(4):
                    act.wait_ge(l_z, 4 * c + s + 1)
                    act.copy(z_sb[0:SUB, s, :], banks[2 + s][0:SUB, 0:D + 2 * HEADS]).then_inc(l_zc, 1)
            pass_act(act, layer1, 1)
            with act.Fori(0, CHUNKS) as c:
                for s in range(4):
                    act.wait_ge(f_mv, 4 * c + s + 1)
                    act.activation(fin_s[0:SUB, s:s + 1], fin_mv[0:SUB, s, 1:2], ACT.Sqrt,
                                   bias=ln_eps[0:SUB, :]).then_inc(f_std, 1)

        @block.vector
        def _(dve):
            def step(ins=None):
                dve.drain()

            dve.wait_ge(consts, 1)
            dve.tensor_copy(iota[:, :], iota_i[:, :])
            dve.memset(mean_w[:, :], 1.0 / D)
            dve.memset(ones_b[:, :], 1.0)
            dve.memset(ln_eps[:, :], LN_EPS)
            dve.memset(bn_eps[:, :], BN_EPS)
            dve.wait_ge(const_in, 16 * 12)
            dve.tensor_copy(b_part[:, 0, :], b_row[:, :])
            step()
            dve.tensor_tensor(b_rest[:, 0, :], b_row[:, :], b_part[:, 0, :], ALU.subtract)
            step()
            dve.tensor_copy(b_part[:, 1, :], b_rest[:, 0, :])
            step()
            dve.tensor_tensor(b_rest[:, 1, :], b_rest[:, 0, :], b_part[:, 1, :], ALU.subtract)
            step()
            dve.tensor_copy(b_part[:, 2, :], b_rest[:, 1, :])
            dve.drain().then_inc(b_split, 1)
            dve.tensor_scalar(eps1[:, :], eps1[:, :], 1.0, None, ALU.add)
            dve.wait_ge(dst_in, 48)
            dve.tensor_copy(first_f[:, :], firsts[:, 0, :])
            dve.tensor_copy(plan[:, 0, :], firsts[0:1, 0, :])
            dve.tensor_tensor(plan[:, 1, :], firsts[0:1, 1, :], firsts[0:1, 0, :], ALU.subtract)
            step()
            dve.tensor_scalar(plan[:, 1, :], plan[:, 1, :], 6, None, ALU.arith_shift_right)
            step()
            dve.tensor_copy(plan_f[:, 0, :], plan[:, 1, :])
            dve.memset(plan_f[:, 1, :], 1.0)
            step()
            dve.tensor_tensor_scan(plan_f[:, 2, :], plan_f[:, 1, :], plan_f[:, 0, :], 0.0, ALU.mult, ALU.add)
            dve.tensor_scalar(plan[:, 1, :], plan_f[:, 0, :], 1.0, None, ALU.add)
            step()
            dve.tensor_tensor(plan[:, 2, :], plan_f[:, 2, :], plan_f[:, 0, :], ALU.subtract)
            dve.tensor_tensor(dst_off[:, :, :], dst_raw[:, :].rearrange("p (g j) -> p g j", j=J),
                              first_f[:, :].unsqueeze(2).to_broadcast([P, GROUPS, J]), ALU.subtract)
            dve.drain().then_inc(planned, 1)
            dve.memset(acc[:, :, :], 0.0)
            dve.drain().then_inc(acc_zeroed, 1)
            pass_vector(dve, layer0, 0)

            for n in range(2):
                for k in range(HALF):
                    dve.tensor_tensor(buf_c[:, k, 0:D], wz[:, k, 0:D], att[:, n, :], ALU.mult)
                    step()
                    dve.tensor_reduce(wz[:, k, D + n * HEADS:D + (n + 1) * HEADS],
                                      buf_c[:, k, 0:D].rearrange("p (h f) -> p h f", h=HEADS), AX.X, ALU.add)
            dve.drain().then_inc(wz_ready, 1)

            def node_sums(c, at, n):
                dve.wait_ge(chunk_x, 16 * c + 16)
                if not isinstance(c, int) or c > 0:
                    dve.wait_ge(a_pe1, c)
                dve.scalar_tensor_tensor(buf_b, buf_a, eps1[:, 0:1], acc[:, :, at], ALU.mult, ALU.add).then_inc(a_hid, 1)
                dve.wait_ge(a_act2, c + 1)
                for k in range(HALF):
                    dve.bn_stats(stats[:, k, bass.ds(c, 1), :].rearrange("p a s -> p (a s)") if not isinstance(c, int)
                                 else stats[:, k, c, :], node_x[:, k, at][:, 0:n])

            with dve.Fori(0, CHUNKS - 1) as c:
                node_sums(c, bass.ds(c * CHUNK, CHUNK), CHUNK)
            node_sums(CHUNKS - 1, slice((CHUNKS - 1) * CHUNK, CHUNKS * CHUNK), TAIL)
            step()
            for k in range(HALF):
                dve.bn_aggr(mv[:, k, :], stats[:, k, :, :].rearrange("p c s -> p (c s)"))
            dve.drain().then_inc(bn_var, 1)
            dve.wait_ge(bn_sqrt, 1)
            dve.reciprocal(bn_shift[:, :], bn_tmp[:, :])
            step()
            dve.tensor_tensor(bn_scale[:, :], bn_shift[:, :], cols[:, 2, :], ALU.mult)
            step()
            dve.tensor_tensor(bn_tmp[:, :], bn_scale[:, :], mv[:, :, 0], ALU.mult)
            step()
            dve.tensor_tensor(bn_shift[:, :], cols[:, 3, :], bn_tmp[:, :], ALU.subtract)
            dve.drain().then_inc(bn_ready, 1)

            with dve.Fori(0, CHUNKS) as c:
                at = bass.ds(c * CHUNK, CHUNK)
                dve.wait_ge(chunk_y, 16 * c + 16)
                dve.wait_ge(l_bn, c + 1)
                dve.tensor_tensor(buf_b, buf_a, buf_c, ALU.add).then_inc(l_res, 1)
                dve.wait_ge(l_mean, c + 1)
                for k in range(HALF):
                    last = dve.tensor_tensor(buf_c[:, k, :], buf_b[:, k, :], banks[0][:, 0:CHUNK], ALU.subtract)
                last.then_inc(l_cen, 1)
                dve.wait_ge(l_std, c + 1)
                dve.reciprocal(rstd, rstd)
                step()
                dve.tensor_tensor(buf_d, buf_c, rstd.unsqueeze(1).to_broadcast([P, HALF, CHUNK]), ALU.mult)
                step()
                dve.tensor_copy(node_x[:, :, at], buf_d)
                dve.drain().then_inc(l_x, 1)

            with dve.Fori(0, GROUPS // 2) as i:
                for u in range(2):
                    g = i * 2 + u
                    a, b = score_rows(u), score_rows(2 + u)
                    e = expo[:, u, :]
                    dve.wait_ge(s_stored[u], 16 * i)
                    dve.wait_ge(s_rows[u], 2 * 16 * J * (i + 1))
                    dve.tensor_tensor(a, a, b, ALU.add)
                    step()
                    dve.scalar_tensor_tensor(b, a, SLOPE, a, ALU.mult, ALU.max)
                    step()
                    dve.tensor_scalar(a, b, 0.0, NEG, ALU.is_equal, ALU.mult)
                    step()
                    dve.tensor_tensor(e, a, b, ALU.add).then_inc(s_score, 1)

            dve.wait_ge(m_in, 64)
            before, here, after = (line_dst(n) for n in range(3))
            dve.tensor_tensor(pen_in, here, before, ALU.not_equal)
            dve.tensor_tensor(pen_out, here, after, ALU.not_equal)
            step()
            dve.tensor_scalar(pen_in, pen_in, FAR, None, ALU.mult)
            dve.tensor_scalar(pen_out, pen_out, FAR, None, ALU.mult)
            dve.memset(carry_t[0:HEADS, :], FAR)
            step()
            e = acc_line(0).rearrange("p (n h) -> p n h", h=HEADS)
            f = acc_line(1).rearrange("p (n h) -> p n h", h=HEADS)
            for n in range(2):
                pen, data, way = ((pen_in, e, slice(None)), (pen_out, f, slice(None, None, -1)))[n]
                end = (LINE - 1, 0)[n]
                for h in range(HEADS):
                    dve.tensor_tensor_scan(run_max[:, way], pen[:, way], data[:, way, h], FAR, ALU.add, ALU.max)
                    step()
                    dve.tensor_copy(lasts[:, h:h + 1], run_max[:, end:end + 1])
                    dve.tensor_reduce(lasts[:, HEADS + h:HEADS + h + 1], pen, AX.X, ALU.min)
                    step()
                dve.drain().then_inc(m_last, 1)
                dve.wait_ge(m_lastT, n + 1)
                dve.tensor_copy(carry_sb[0:HEADS, :], banks[0][0:HEADS, 0:2 * P])
                step()
                dve.tensor_tensor_scan(carry_t[0:HEADS, 1:P + 1][:, way], carry_sb[0:HEADS, P:2 * P][:, way],
                                       carry_sb[0:HEADS, 0:P][:, way], FAR, ALU.add, ALU.max)
                step()
                if n == 1:
                    dve.tensor_copy(carry_sb[0:HEADS, 0:P], carry_t[0:HEADS, 1:P + 1])
                    step()
                    dve.memset(carry_t[0:HEADS, P:P + 1], FAR)
                    dve.tensor_copy(carry_t[0:HEADS, 1:P], carry_sb[0:HEADS, 1:P])
                    step()
                dve.drain().then_inc(m_carry, 1)
                dve.wait_ge(m_carryT, n + 1)
                dve.tensor_copy(carry[:, 0:HEADS], banks[1][:, 0:HEADS])
                step()
                for h in range(HEADS):
                    out = f[:, :, h] if n == 0 else run_max
                    dve.tensor_tensor_scan(out[:, way], pen[:, way], data[:, way, h], carry[:, h:h + 1],
                                           ALU.add, ALU.max)
                    step()
                    if n == 1:
                        dve.tensor_tensor(e[:, :, h], e[:, :, h], run_max, ALU.subtract)
                        step()
            dve.tensor_scalar(acc_line(0), acc_line(0), FLOOR, None, ALU.max).then_inc(m_done, 1)
            dve.wait_ge(layer1.acc_zero, 1)
            pass_vector(dve, layer1, 1)

            dve.drain()
            with dve.Fori(0, CHUNKS) as c:
                at = bass.ds(c * CHUNK, CHUNK)
                dve.wait_ge(f_spread, c)
                dve.tensor_scalar(rstd[0:HEADS, :], den[:, at], 0.0, None, ALU.is_le)
                step()
                dve.tensor_tensor(rstd[0:HEADS, :], rstd[0:HEADS, :], den[:, at], ALU.add)
                step()
                dve.reciprocal(rstd[0:HEADS, :], rstd[0:HEADS, :]).then_inc(f_rden, 1)
                dve.wait_ge(f_spread, c + 1)
                dve.wait_ge(f_turn, 4 * c)
                for k in range(HALF):
                    dve.tensor_tensor(buf_b[:, k, :], acc[:, k, at], banks[k][:, 0:CHUNK], ALU.mult)
                step()
                dve.tensor_tensor(buf_b, buf_b, node_x[:, :, at], ALU.add).then_inc(f_sum, 1)
                dve.wait_ge(f_out, 16 * c)
                for s in range(4):
                    x = banks[2 + s][0:SUB, 0:D]
                    dve.wait_ge(f_turn, 4 * c + s + 1)
                    dve.bn_stats(fin_stats[0:SUB, s, :], x)
                    step()
                    dve.bn_aggr(fin_mv[0:SUB, s, :], fin_stats[0:SUB, s, :])
                    dve.drain().then_inc(f_mv, 1)
                for s in range(4):
                    x = banks[2 + s][0:SUB, 0:D]
                    dve.wait_ge(f_std, 4 * c + s + 1)
                    dve.reciprocal(fin_r[0:SUB, s:s + 1], fin_s[0:SUB, s:s + 1])
                    step()
                    dve.tensor_scalar(fin[0:SUB, s, :], x, fin_mv[0:SUB, s, 0:1], fin_r[0:SUB, s:s + 1],
                                      ALU.subtract, ALU.mult).then_inc(f_nrm, 1)


def kernel(x, src, dst, edge_attr_128, L0_gnn_W_edge, L0_gnn_b_edge, L0_gnn_W1, L0_gnn_b1, L0_gnn_W2, L0_gnn_b2,
           L0_gnn_eps, L0_gnn_gamma, L0_gnn_beta, L1_gnn_W, L1_gnn_att):
    import numpy as np
    import concourse.bacc as bacc
    from concourse.bass_utils import run_bass_kernel_spmd

    x, edge = np.asarray(x), np.asarray(edge_attr_128)
    pad = EPAD - EDGES
    src_p = np.concatenate([np.asarray(src), np.zeros(pad, np.int32)])
    dst_p = np.concatenate([np.asarray(dst), np.full(pad, NODES, np.int32)])
    edge_p = np.concatenate([edge, np.zeros((pad, EDGE_D), edge.dtype)])
    x_t = np.zeros((D, NPAD), x.dtype)
    x_t[:, :NODES] = x.T
    by_half = lambda w: np.ascontiguousarray(np.asarray(w).reshape(HALF, P, -1).transpose(1, 0, 2))
    by_col = lambda v: np.ascontiguousarray(np.asarray(v).reshape(HALF, P).T)
    att = np.asarray(L1_gnn_att)
    end = np.full(1, -1, np.int32)
    arrays = {
        "x": x,
        "src_idx": src_p.reshape(GROUPS, P, J),
        "dst_idx": dst_p.reshape(GROUPS, P, J),
        "dst_pm": dst_p.reshape(GROUPS, P, J).transpose(1, 0, 2).reshape(P, GROUPS * J),
        "dst_ext": np.concatenate([end, dst_p, end]).reshape(1, EPAD + 2),
        "first": dst_p[::GROUP].reshape(1, GROUPS),
        "last": dst_p[GROUP - 1::GROUP].reshape(1, GROUPS),
        "edge_t": edge_p.reshape(GROUPS, P, J, EDGE_D).transpose(0, 3, 2, 1).reshape(GROUPS, EDGE_D, GROUP),
        "x_t": by_half(x_t),
        "w_edge": np.asarray(L0_gnn_W_edge),
        "b_edge": np.asarray(L0_gnn_b_edge).reshape(1, D),
        "w1": by_half(L0_gnn_W1), "w2": by_half(L0_gnn_W2),
        "b1": by_col(L0_gnn_b1), "b2": by_col(L0_gnn_b2),
        "gamma": by_col(L0_gnn_gamma), "beta": by_col(L0_gnn_beta),
        "eps": np.asarray(L0_gnn_eps).reshape(1, 1),
        "wz": by_half(np.asarray(L1_gnn_W).transpose(1, 0, 2).reshape(D, D)),
        "att_src": att[:, :HEAD_D].reshape(1, D), "att_dst": att[:, HEAD_D:].reshape(1, D),
    }
    nc = bacc.Bacc("TRN2", target_bir_lowering=False, num_devices=1)
    feeds, t = {}, {}
    for name, a in arrays.items():
        a = np.ascontiguousarray(a)
        feeds[f"in_{name}"] = a
        t[name] = nc.dram_tensor(f"in_{name}", a.shape, mybir.dt.from_np(a.dtype), kind="ExternalInput").ap()
    t["out"] = nc.dram_tensor("out_0", (NODES, D), F32, kind="ExternalOutput").ap()
    build(nc, t)
    r = run_bass_kernel_spmd(nc, [feeds], core_ids=[0])
    return r.results[0]["out_0"]
```

```python
from contextlib import ExitStack

import concourse.bass as bass
from concourse import mybir

ALU = mybir.AluOpType
ACT = mybir.ActivationFunctionType
AX = mybir.AxisListType
F32 = mybir.dt.float32
BF16 = mybir.dt.bfloat16
I32 = mybir.dt.int32

P = 128
NODES = 6250
EDGES = 200000
D = 256
HALF = D // P
EDGE_D = 128
HEADS = 4
HEAD_D = D // HEADS
J = 8
GROUP = P * J
GROUPS = -(-EDGES // GROUP)
EPAD = GROUPS * GROUP
RING = 4
ROUNDS = GROUPS // RING
PAIRS = J // 2
WIN = 128
ROW = D + HEADS
CHUNK = 448
CHUNKS = -(-NODES // CHUNK)
NPAD = CHUNK * CHUNKS
TAIL = NODES - CHUNK * (CHUNKS - 1)
SUB = CHUNK // 4
ACC_W = NPAD + WIN
LINE = EPAD // P
BN_EPS = 1e-5
LN_EPS = 1e-5
SLOPE = 0.01
NEG = -1000.0
FAR = -1e30
FLOOR = -80.0
ES_LIMIT = 19.0
NEG_NEAR = -40.0
PARTS = 3


def build(nc, t):
    with ExitStack() as ctx:
        def sb(name, shape, dt=F32):
            return ctx.enter_context(nc.sbuf_tensor(name, shape, dt))

        def sem(name):
            return ctx.enter_context(nc.semaphore(name))

        def dram(name, shape, dt=F32):
            return nc.dram_tensor(name, shape, dt).ap()

        z_tab = dram("z_tab", (NPAD, ROW))
        es_tab = dram("es_tab", (NPAD, HEADS))
        ed_tab = dram("ed_tab", (NPAD, HEADS))
        ed_parts = dram("ed_parts", (NPAD + WIN, PARTS * HEADS), BF16)
        score_tab = dram("score_tab", (GROUPS, P, J * HEADS))
        expo_tab = dram("expo_tab", (GROUPS, P, J * HEADS))

        acc = sb("acc", [P, HALF, ACC_W])
        node_x = sb("node_x", [P, HALF, NPAD])
        rows = sb("rows", [P, RING, J, ROW])
        edge_room = sb("edge_room", [P, ACC_W])
        edge_in = edge_room[:, 0:RING * GROUP].rearrange("p (r n) -> p r n", r=RING)
        den = edge_room[0:HEADS, :]
        onehot = sb("onehot", [P, 3, J, WIN])
        idx = sb("idx", [P, RING, J], I32)
        dst_off = sb("dst_off", [P, GROUPS, J])
        off_here = sb("off_here", [P, J])
        first_f = sb("first_f", [P, GROUPS])
        node_at = sb("node_at", [P, GROUPS])
        dst_t = sb("dst_t", [P, 2, GROUP], I32)
        hot_t = sb("hot_t", [P, GROUP], BF16)
        ed_win = sb("ed_win", [P, RING, PARTS * HEADS], BF16)
        score = sb("score", [P, 3, J * HEADS])
        lrelu = sb("lrelu", [P, 2, J * HEADS])
        es_max = sb("es_max", [P, 2, 4 * HEADS])
        ed_split = sb("ed_split", [P, 4, PARTS, HEADS], BF16)
        ed_rest = sb("ed_rest", [P, 2, 4, HEADS])
        es_top = sb("es_top", [P, 1])
        choice = sb("choice", [1, 4])
        mode = sb("mode", [1, 1], I32)
        zero_b = sb("zero_b", [P, PARTS * HEADS], BF16)
        part_i = sb("part_i", [P, 1], I32)
        part = sb("part", [P, 1])
        ones_row = sb("ones_row", [1, P])
        plan = sb("plan", [1, 3, GROUPS], I32)
        agg_sb = sb("agg_sb", [WIN, ROW])
        expo = sb("expo", [P, RING, J * HEADS])
        iota_i = sb("iota_i", [P, WIN], I32)
        iota = sb("iota", [P, WIN])
        ident = sb("ident", [P, P])
        mean_w = sb("mean_w", [P, P])
        ones_b = sb("ones_b", [3, P], BF16)
        w_edge = sb("w_edge", [P, D])
        b_three = sb("b_three", [3, D], BF16)
        w1 = sb("w1", [P, HALF, D])
        w2 = sb("w2", [P, HALF, D])
        wz = sb("wz", [P, HALF, D + 2 * HEADS])
        cols = sb("cols", [P, 4, HALF])
        eps1 = sb("eps1", [P, 1])
        ln_eps = sb("ln_eps", [P, 1])
        bn_eps = sb("bn_eps", [P, 1])
        stats = sb("stats", [P, HALF, CHUNKS, 6])
        mv = sb("mv", [P, HALF, 2])
        bn_scale = sb("bn_scale", [P, HALF])
        bn_shift = sb("bn_shift", [P, HALF])
        bn_tmp = sb("bn_tmp", [P, HALF])
        head_sel = sb("head_sel", [HEADS, HALF, P])

        early = node_x[:, :, :].rearrange("p k n -> p (k n)")
        b_row = early[0:1, 0:D]
        b_rest = early[0:1, 2 * D:4 * D].rearrange("p (a n) -> p a n", a=2)
        b_part = early[0:1, 4 * D:4 * D + 3 * D // 2].bitcast(BF16).rearrange("p (a n) -> p a n", a=3)
        att = early[:, 10 * D:12 * D].rearrange("p (a n) -> p a n", a=2)

        dst_raw = early[:, 12 * D:12 * D + GROUPS * J].bitcast(I32)

        firsts = early[:, 20 * D:20 * D + 2 * GROUPS].bitcast(I32).rearrange("p (a n) -> p a n", a=2)
        plan_f = early[0:1, 24 * D:24 * D + 3 * GROUPS].rearrange("p (a n) -> p a n", a=3)

        spare = rows[:, :, :, :].rearrange("p r j c -> p (r j c)")

        def piece(n, width=HALF * CHUNK):
            return spare[:, n * HALF * CHUNK:n * HALF * CHUNK + width]

        def halves(ap):
            return ap.rearrange("p (k n) -> p k n", k=HALF)

        buf_a, buf_b, buf_c, buf_d = (halves(piece(n)) for n in range(4))
        z_sb = piece(4, 4 * (D + 2 * HEADS)).rearrange("p (s c) -> p s c", s=4)
        rstd = piece(6, CHUNK)
        fin = piece(4, 4 * D).rearrange("p (s c) -> p s c", s=4)
        after_rstd = spare[:, 6 * HALF * CHUNK + CHUNK:]
        fin_stats = after_rstd[:, 0:24].rearrange("p (s c) -> p s c", s=4)
        fin_mv = after_rstd[:, 24:32].rearrange("p (s c) -> p s c", s=4)
        fin_r, fin_s = after_rstd[:, 32:36], after_rstd[:, 36:40]

        flat = acc[:, :, :].rearrange("p k n -> p (k n)")

        def acc_line(n):
            return flat[:, n * LINE * HEADS:(n + 1) * LINE * HEADS]

        def line_dst(n):
            return spare[:, n * LINE:(n + 1) * LINE].bitcast(I32)

        pen_in, pen_out = (spare[:, n * LINE:(n + 1) * LINE] for n in (3, 4))
        edge_flat = edge_room
        run_max = edge_flat[:, 0:LINE]
        lasts = edge_flat[:, LINE:LINE + 16]
        carry_t = edge_flat[:, LINE + 16:LINE + 16 + 2 * P + 2]
        carry = edge_flat[:, LINE + 300:LINE + 300 + 2 * HEADS]
        carry_sb = edge_flat[:, LINE + 320:LINE + 320 + 2 * P]

        def score_rows(n):
            return spare[:, n * J * HEADS:(n + 1) * J * HEADS]

        banks = [ctx.enter_context(nc.psum_tensor(f"bank{n}", [P, 512], F32)) for n in range(8)]
        agg_ps, turn_ps = banks[4], banks[5]

        const_in = sem("const_in")
        dst_in = sem("dst_in")
        passed = sem("passed")
        consts = sem("consts")
        acc_zeroed = sem("acc_zeroed")
        planned = sem("planned")
        b_split = sem("b_split")
        b_in = sem("b_in")

        class Layer:
            def __init__(self, n):
                s = lambda name: sem(f"{name}{n}")
                self.idx_in = [s(f"idx_in_{u}_") for u in range(RING)]
                self.rows_in = [s(f"rows_in_{u}_") for u in range(RING)]
                self.edge_in = [s(f"edge_in_{u}_") for u in range(RING)]
                self.edge_done, self.summed, self.msg_ready = s("edge_done"), s("summed"), s("msg_ready")
                self.onehot_ready, self.agg_ready, self.agg_copied = s("onehot"), s("agg"), s("aggc")
                self.turned, self.group_done = s("turned"), s("group_done")
                self.x_onehot, self.x_agg, self.x_copied = s("x_onehot"), s("x_agg"), s("x_copied")
                self.x_turned, self.x_added = s("x_turned"), s("x_added")
                self.acc_zero = s("acc_zero")
                self.spread_hot, self.scored = s("spread_hot"), s("scored")
                self.ed_in = [s(f"ed_in_{u}_") for u in range(RING)] if n else []
                self.dst_in = [s(f"dst_in_{u}_") for u in range(2)] if n else []

        layer0, layer1 = Layer(0), Layer(1)

        chunk_x = sem("chunk_x")
        a_hid, a_pe1, a_act1, a_pe2, a_act2, a_stat = (sem(f"a_{x}") for x in ("h", "p1", "r1", "p2", "r2", "st"))
        bn_ready = sem("bn_ready")
        bn_sqrt = sem("bn_sqrt")
        bn_var = sem("bn_var")
        chunk_y = sem("chunk_y")
        l_bn, l_res, l_mean, l_cen, l_sq, l_var, l_std, l_x, l_z, l_zc, l_out = (
            sem(f"l_{x}") for x in ("bn", "res", "mean", "cen", "sq", "var", "std", "x", "z", "zc", "out"))
        wz_ready = sem("wz_ready")
        l_split, l_tail, top_ready, top_turned, top_one, top_all, mode_ready = (
            sem(f"l_{x}") for x in ("split", "tail", "top", "topT", "top1", "topA", "mode"))
        att_ready = sem("att_ready")
        s_idx = [sem(f"s_idx{u}") for u in range(2)]
        s_rows = [sem(f"s_rows{u}") for u in range(2)]
        s_score = sem("s_score")
        s_stored = [sem(f"s_stored{u}") for u in range(2)]
        m_in = sem("m_in")
        m_pen = sem("m_pen")
        m_last, m_lastT, m_carry, m_carryT = (sem(f"m_{x}") for x in ("last", "lastT", "carry", "carryT"))
        m_done = sem("m_done")
        m_out = sem("m_out")
        f_rden, f_spread, f_sum, f_turn, f_mv, f_std, f_r, f_nrm, f_out = (
            sem(f"f_{x}") for x in ("rden", "spread", "sum", "turn", "mv", "std", "r", "nrm", "out"))

        block = ctx.enter_context(nc.Block())


        def rounds(eng, body, peel_last=False):
            for u in range(RING):
                body(0, u, u)
            with eng.Fori(1, ROUNDS - peel_last) as i:
                for u in range(RING):
                    body(i, u, i * RING + u)
            if peel_last:
                for u in range(RING):
                    body(ROUNDS - 1, u, (ROUNDS - 1) * RING + u)

        def first_round(i):
            return isinstance(i, int) and i == 0

        def after_last(g):
            return isinstance(g, int) and g >= GROUPS

        def pass_loads(sp, L, layer, fast=False):
            def body(i, u, g):
                if not first_round(i):
                    sp.wait_ge(L.rows_in[u], 16 * J * i)
                sp.dma_start(idx[:, u, :], t["src_idx"][g]).then_inc(L.idx_in[u], 16)
                if layer == 0:
                    if not first_round(i):
                        sp.wait_ge(L.edge_done, PAIRS * (g - RING + 1))
                    sp.dma_start(edge_in[:, u, :], t["edge_t"][g]).then_inc(L.edge_in[u], 16)
                elif fast:
                    base = sp.value_load(plan[0:1, 0, bass.ds(g, 1)], min_val=0, max_val=NODES)
                    if not (first_round(i) and g < 2):
                        sp.wait_ge(L.spread_hot, g - 1)
                        sp.sem_inc(passed, 1)
                    sp.dma_start(dst_t[:, u % 2, :], t["dst_jp"][g].to_broadcast([P, GROUP])).then_inc(L.dst_in[u % 2], 16)
                    if not first_round(i):
                        sp.wait_ge(L.edge_done, g - RING + 1)
                    sp.sem_inc(passed, 1)
                    sp.dma_start(ed_win[:, u, :], ed_parts[bass.ds(base, WIN), :]).then_inc(L.ed_in[u], 16)
                else:
                    if not first_round(i):
                        sp.wait_ge(L.group_done, g - RING + 1)
                    sp.dma_start(expo[:, u, :], expo_tab[g]).then_inc(L.edge_in[u], 16)
            rounds(sp, body)

        def pass_gathers(pool, L, layer):
            table, width = (t["x"], D) if layer == 0 else (z_tab, ROW)

            def body(i, u, g):
                if not first_round(i):
                    pool.wait_ge(L.group_done, g - RING + 1)
                    pool.sem_inc(passed, 1)
                pool.wait_ge(L.idx_in[u], 16 * i + 16)
                if not first_round(i):
                    pool.sem_inc(passed, 1)
                for j in range(J):
                    nc.gpsimd.indirect_dma_start(
                        rows[:, u, j, 0:width], None, table,
                        bass.IndirectOffsetOnAxis(ap=idx[:, u, j:j + 1], axis=0)).then_inc(L.rows_in[u], 16)
            rounds(pool, body)

        def turn(pe, L, dst_sem):
            pe.sem_inc(passed, 1)
            for k in range(HALF):
                last = pe.transpose(turn_ps[:, k * WIN:(k + 1) * WIN], agg_sb[:, k * P:(k + 1) * P],
                                    ident[:, :])
            if L is layer1:
                last = pe.transpose(turn_ps[0:HEADS, HALF * WIN:(HALF + 1) * WIN], agg_sb[:, D:ROW],
                                    ident[:, :])
            last.then_inc(dst_sem, 1)

        def pass_matmuls(pe, L, layer, fast=False):
            width = D if layer == 0 else ROW
            msgs = PAIRS if layer == 0 else 2

            def edge_products(i, u, g, pairs):
                for q in pairs:
                    if q == 0:
                        pe.wait_ge(L.edge_in[u], 16 * i + 16)
                    if not (first_round(i) and g == 0):
                        pe.wait_ge(L.summed, PAIRS * (g - 1) + q + 1)
                    for h in range(2):
                        j = 2 * q + h
                        out = banks[q][:, h * D:(h + 1) * D]
                        pe.matmul(out, ones_b[:, :], b_three[:, :], start=True, stop=False)
                        last = pe.matmul(out, edge_in[:, u, j * P:(j + 1) * P], w_edge[:, :], start=False, stop=True)
                    last.then_inc(L.edge_done, 1)

            def spread_ed(i, u, g):
                if after_last(g):
                    return
                pe.wait_ge(L.spread_hot, g + 1)
                pe.wait_ge(L.ed_in[u % RING], 16 * (i + u // RING) + 16)
                for j in range(J):
                    last = pe.matmul(banks[u % 2][:, j * PARTS * HEADS:(j + 1) * PARTS * HEADS],
                                     hot_t[:, j * P:(j + 1) * P], ed_win[:, u % RING, :], start=True, stop=True)
                last.then_inc(L.edge_done, 1)

            def sum_window(hot, u, dst_sem):
                for j in range(J):
                    last = pe.matmul(agg_ps[0:WIN, 0:width], onehot[:, hot, j, :], rows[:, u, j, 0:width],
                                     start=(j == 0), stop=(j == J - 1))
                last.then_inc(dst_sem, 1)

            def sum_first(u, g):
                pe.wait_ge(L.onehot_ready, g + 1)
                pe.wait_ge(L.msg_ready, msgs * (g + 1))
                sum_window(u % 2, u, L.agg_ready)

            def turn_first(g, at_start):
                pe.wait_ge(L.agg_copied, g + 1)
                if not at_start:
                    pe.wait_ge(L.group_done, g)
                turn(pe, L, L.turned)

            def extras(u, g):
                windows = pe.value_load(plan[0:1, 1, bass.ds(g, 1)], min_val=1, max_val=CHUNKS * 8)
                before = pe.value_load(plan[0:1, 2, bass.ds(g, 1)], min_val=0, max_val=1 << 20)
                with pe.If(windows > 1):
                    with pe.Fori(1, windows) as k:
                        pe.wait_ge(L.x_onehot, before + k)
                        sum_window(2, u, L.x_agg)
                        pe.wait_ge(L.x_copied, before + k)
                        turn(pe, L, L.x_turned)

            def body(i, u, g):
                n = g if first_round(i) else RING
                if layer == 0:
                    edge_products(i, u, g, range(PAIRS - 1))
                if n >= 2 and not fast:
                    extras((u - 2) % RING, g - 2)
                if n >= 1:
                    sum_first((u - 1) % RING, g - 1)
                if layer == 0:
                    edge_products(i, u, g, range(PAIRS - 1, PAIRS))
                if n >= 1:
                    turn_first(g - 1, n == 1)
                if fast:
                    spread_ed(i, u + 1, g + 1)
            if fast:
                spread_ed(0, 0, 0)
            rounds(pe, body, peel_last=fast)
            if not fast:
                extras(RING - 2, GROUPS - 2)
            sum_first(RING - 1, GROUPS - 1)
            turn_first(GROUPS - 1, False)
            if not fast:
                extras(RING - 1, GROUPS - 1)

        def pass_act(act, L, layer, fast=False):
            width = D if layer == 0 else ROW

            def copy_window(dst_sem):
                act.copy(agg_sb[:, 0:width], agg_ps[0:WIN, 0:width]).then_inc(dst_sem, 1)

            def copy_first(g, at_start):
                act.wait_ge(L.agg_ready, g + 1)
                if not at_start:
                    act.wait_ge(L.group_done, g)
                copy_window(L.agg_copied)

            def extras(g):
                windows = act.value_load(plan[0:1, 1, bass.ds(g, 1)], min_val=1, max_val=CHUNKS * 8)
                before = act.value_load(plan[0:1, 2, bass.ds(g, 1)], min_val=0, max_val=1 << 20)
                with act.If(windows > 1):
                    with act.Fori(1, windows) as k:
                        act.wait_ge(L.x_agg, before + k)
                        copy_window(L.x_copied)

            def body(i, u, g):
                start = first_round(i) and g == 0
                if layer == 0:
                    for q in range(PAIRS):
                        if q == PAIRS - 1 and not start:
                            copy_first(g - 1, first_round(i) and g == 1)
                        act.wait_ge(L.summed, PAIRS * g + q + 1)
                        pair = rows[:, u, 2 * q:2 * q + 2, 0:D]
                        act.activation(pair, pair, ACT.Relu).then_inc(L.msg_ready, 1)
                else:
                    if fast:
                        act.wait_ge(L.scored, g + 1)
                    else:
                        act.wait_ge(L.edge_in[u], 16 * i + 16)
                        act.wait_ge(L.rows_in[u], 16 * J * (i + 1))
                    act.activation(rows[:, u, :, D:ROW], expo[:, u, :].rearrange("p (j h) -> p j h", j=J),
                                   ACT.Exp).then_inc(L.summed, 1)
                    if not start:
                        copy_first(g - 1, first_round(i) and g == 1)
                if not start and not fast:
                    extras(g - 1)
            rounds(act, body)
            copy_first(GROUPS - 1, False)
            if not fast:
                extras(GROUPS - 1)

        def pass_vector(dve, L, layer, fast=False):
            window_base = dve.alloc_register(f"window_base{layer}{fast}")

            def score_edges(i, u, g):
                js = lambda ap: ap.rearrange("p (j h) -> p j h", j=J)
                parts = banks[u % 2][:, 0:J * PARTS * HEADS].rearrange("p (j q h) -> p j h q", j=J, q=PARTS)
                dve.wait_ge(L.edge_done, g + 1)
                dve.tensor_reduce(js(score[:, 2, :]), parts, AX.X, ALU.add)
                dve.drain()
                dve.wait_ge(L.rows_in[u], 16 * J * (i + 1))
                dve.tensor_tensor(js(score[:, 0, :]), js(score[:, 2, :]), rows[:, u, :, D:ROW], ALU.add)
                dve.tensor_scalar(score[:, 1, :], score[:, 2, :], es_top[:, 0:1], None, ALU.add)
                dve.drain()
                dve.scalar_tensor_tensor(lrelu[:, :, :], score[:, 0:2, :], SLOPE, score[:, 0:2, :], ALU.mult, ALU.max)
                dve.drain()
                dve.tensor_scalar(score[:, 2, :], lrelu[:, 0, :], 0.0, NEG_NEAR, ALU.is_equal, ALU.mult)
                dve.tensor_tensor(score[:, 0, :], lrelu[:, 0, :], lrelu[:, 1, :], ALU.subtract)
                dve.drain()
                dve.tensor_tensor(expo[:, u, :], score[:, 0, :], score[:, 2, :], ALU.add).then_inc(L.scored, 1)

            def add_window(base):
                at = bass.ds(base, WIN)
                last = dve.tensor_tensor(acc[:, :, at], acc[:, :, at],
                                         turn_ps[:, 0:HALF * WIN].rearrange("p (k n) -> p k n", k=HALF), ALU.add)
                if layer == 1:
                    last = dve.tensor_tensor(den[:, at], den[:, at],
                                             turn_ps[0:HEADS, HALF * WIN:(HALF + 1) * WIN], ALU.add)
                return last

            def make_hot_t(i, u, g):
                if after_last(g):
                    return
                dve.wait_ge(L.dst_in[u % 2], 32 * i + 16 * (u // 2) + 16)
                if not (isinstance(g, int) and g == 0):
                    dve.wait_ge(L.edge_done, g)
                dve.tensor_scalar(hot_t[:, :], dst_t[:, u % 2, :], node_at[:, bass.ds(g, 1)], None,
                                  ALU.is_equal).then_inc(L.spread_hot, 1)

            def finish(u, g):
                base = dve.value_load(plan[0:1, 0, bass.ds(g, 1)], min_val=0, max_val=NODES)
                if fast:
                    dve.wait_ge(L.turned, g + 1)
                    add_window(base)
                    dve.drain().then_inc(L.group_done, 1)
                    return
                windows = dve.value_load(plan[0:1, 1, bass.ds(g, 1)], min_val=1, max_val=CHUNKS * 8)
                before = dve.value_load(plan[0:1, 2, bass.ds(g, 1)], min_val=0, max_val=1 << 20)
                dve.wait_ge(L.turned, g + 1)
                add_window(base)
                with dve.If(windows > 1):
                    dve.tensor_copy(off_here[:, :], offsets(g))
                    with dve.Fori(1, windows) as k:
                        dve.drain()
                        dve.tensor_scalar(off_here[:, :], off_here[:, :], float(WIN), None, ALU.subtract)
                        dve.drain()
                        make_onehot(2, off_here[:, :], L.x_onehot)
                        dve.wait_ge(L.x_turned, before + k)
                        dve.reg_mov(window_base, base + k * WIN)
                        add_window(dve.snap(window_base, min_val=0, max_val=NODES))
                dve.drain().then_inc(L.group_done, 1)

            def offsets(g):
                return dst_off[:, bass.ds(g, 1), :].rearrange("p g j -> p (g j)")

            def make_onehot(hot, off, dst_sem):
                dve.tensor_tensor(onehot[:, hot, :, :], off.unsqueeze(2).to_broadcast([P, J, WIN]),
                                  iota[:, :].unsqueeze(1).to_broadcast([P, J, WIN]), ALU.is_equal).then_inc(dst_sem, 1)

            def body(i, u, g):
                make_onehot(u % 2, offsets(g), L.onehot_ready)
                if layer == 0:
                    dve.wait_ge(L.rows_in[u], 16 * J * (i + 1))
                    for q in range(PAIRS):
                        dve.wait_ge(L.edge_done, PAIRS * g + q + 1)
                        pair = rows[:, u, 2 * q:2 * q + 2, 0:D]
                        dve.tensor_tensor(pair, pair, banks[q][:, :].rearrange("p (j d) -> p j d", j=2),
                                          ALU.add).then_inc(L.summed, 1)
                else:
                    if fast:
                        score_edges(i, u, g)
                    dve.wait_ge(L.summed, g + 1)
                    for q in range(2):
                        js = slice(q * J // 2, (q + 1) * J // 2)
                        z = rows[:, u, js, 0:D].rearrange("p j (h f) -> p j h f", h=HEADS)
                        w = rows[:, u, js, D:ROW].unsqueeze(3).to_broadcast([P, J // 2, HEADS, HEAD_D])
                        dve.tensor_tensor(z, z, w, ALU.mult).then_inc(L.msg_ready, 1)
                if fast:
                    make_hot_t(i, u + 1, g + 1)
                if not (first_round(i) and g == 0):
                    finish((u - 1) % RING, g - 1)
            if fast:
                make_hot_t(0, 0, 0)
            rounds(dve, body, peel_last=fast)
            finish(RING - 1, GROUPS - 1)

        @block.sync
        def _(sp):
            for out, of in ((w_edge[:, :], t["w_edge"]), (b_row, t["b_edge"]),
                            (eps1[:, :], t["eps"].to_broadcast([P, 1])),
                            (cols[:, 0, :], t["b1"]), (cols[:, 1, :], t["b2"]),
                            (cols[:, 2, :], t["gamma"]), (cols[:, 3, :], t["beta"]),
                            (w1[:, :, :], t["w1"]), (w2[:, :, :], t["w2"]), (wz[:, :, 0:D], t["wz"]),
                            (att[:, 0, :], t["att_src"].to_broadcast([P, D])),
                            (att[:, 1, :], t["att_dst"].to_broadcast([P, D])),):
                sp.dma_start(out, of).then_inc(const_in, 16)
            sp.dma_start(firsts[:, 0, :], t["first"].to_broadcast([P, GROUPS])).then_inc(dst_in, 16)
            sp.dma_start(firsts[:, 1, :], t["last"].to_broadcast([P, GROUPS])).then_inc(dst_in, 16)
            sp.dma_start(dst_raw[:, :], t["dst_pm"]).then_inc(dst_in, 16)
            sp.wait_ge(b_split, 1)
            for n in range(3):
                sp.dma_start(b_three[n:n + 1, :], b_part[:, n, :]).then_inc(b_in, 16)
            pass_loads(sp, layer0, 0)

            sp.wait_ge(layer0.group_done, GROUPS)
            with sp.Fori(0, CHUNKS) as c:
                sp.wait_ge(a_hid, c)
                sp.dma_start(buf_a, t["x_t"][:, :, bass.ds(c * CHUNK, CHUNK)]).then_inc(chunk_x, 16)
            sp.wait_ge(a_hid, CHUNKS)
            sp.wait_ge(acc_zeroed, 1)
            sp.dma_start(ed_parts[NPAD:NPAD + WIN, :], zero_b[:, :]).then_inc(l_tail, 16)
            with sp.Fori(0, CHUNKS) as c:
                sp.wait_ge(l_res, c)
                sp.dma_start(buf_a, t["x_t"][:, :, bass.ds(c * CHUNK, CHUNK)]).then_inc(chunk_y, 16)
                at = bass.ds(c * CHUNK, CHUNK)
                sp.wait_ge(l_split, c + 1)
                sp.dma_start(ed_parts[at, :].rearrange("(s p) c -> p s c", s=4),
                             ed_split[0:SUB, :, :, :].rearrange("p s q h -> p s (q h)")).then_inc(l_out, 16)
                for tab, lo, hi in ((z_tab, 0, ROW), (es_tab, D, D + HEADS), (ed_tab, D + HEADS, D + 2 * HEADS)):
                    sp.dma_start(tab[at, :].rearrange("(s p) c -> p s c", s=4), z_sb[0:SUB, :, lo:hi]).then_inc(l_out, 16)
            sp.wait_ge(l_out, 64 * CHUNKS)

            sp.wait_ge(l_tail, 16)
            sp.wait_ge(mode_ready, 1)
            bounded = sp.value_load(mode[0:1, 0:1], min_val=0, max_val=1)
            with sp.If(bounded > 0):
                pass_loads(sp, layer1, 1, fast=True)
            with sp.Else():
                with sp.Fori(0, GROUPS // 2) as i:
                    for u in range(2):
                        g = i * 2 + u
                        sp.wait_ge(s_rows[u], 2 * 16 * J * i)
                        sp.dma_start(idx[:, u, :], t["src_idx"][g]).then_inc(s_idx[u], 16)
                        sp.dma_start(idx[:, 2 + u, :], t["dst_idx"][g]).then_inc(s_idx[u], 16)
                    for u in range(2):
                        g = i * 2 + u
                        sp.wait_ge(s_score, g + 1)
                        sp.dma_start(score_tab[g], expo[:, u, :]).then_inc(s_stored[u], 16)
                for u in range(2):
                    sp.wait_ge(s_stored[u], 16 * (GROUPS // 2))
                line = score_tab.rearrange("g p c -> (g p c)").rearrange("(q n) -> q n", q=P)
                sp.dma_start(acc_line(0), line).then_inc(m_in, 16)
                for n in range(3):
                    sp.dma_start(line_dst(n), t["dst_ext"][:, n:n + EPAD].rearrange("a (q n) -> (a q) n", q=P)).then_inc(m_in, 16)
                sp.wait_ge(m_done, 1)
                oline = expo_tab.rearrange("g p c -> (g p c)").rearrange("(q n) -> q n", q=P)
                sp.dma_start(oline, acc_line(0)).then_inc(m_out, 16)
                sp.wait_ge(m_out, 16)
                pass_loads(sp, layer1, 1)

            def store(c, at, n):
                sp.wait_ge(f_nrm, c * 4 + 4)
                whole = n // SUB
                sp.dma_start(t["out"][bass.ds(c * CHUNK, whole * SUB), :]
                             .rearrange("(s p) c -> p s c", s=whole), fin[0:SUB, 0:whole, :]).then_inc(f_out, 16)
                if n > whole * SUB:
                    rest = n - whole * SUB
                    sp.dma_start(t["out"][c * CHUNK + whole * SUB:c * CHUNK + n, :], fin[0:rest, whole, :]).then_inc(f_out, 16)

            with sp.Fori(0, CHUNKS - 1) as c:
                store(c, None, CHUNK)
            store(CHUNKS - 1, None, TAIL)
            sp.wait_ge(f_out, 16 * (CHUNKS + 1))

        @block.gpsimd
        def _(pool):
            nc.gpsimd.iota(iota_i[:, :], pattern=[[1, WIN]], base=0, channel_multiplier=0).then_inc(consts, 1)
            nc.gpsimd.memset(ident[:, :], 0.0)
            nc.gpsimd.memset(head_sel[:, :, :], 1.0)
            pool.drain()
            nc.gpsimd.affine_select(out=ident[:, :], in_=ident[:, :], compare_op=ALU.not_equal, fill=1.0, base=0,
                                    pattern=[[-1, P]], channel_multiplier=1)
            sel = head_sel[:, :, :]
            nc.gpsimd.affine_select(out=sel, in_=sel, compare_op=ALU.is_ge, fill=0.0, base=0,
                                    pattern=[[P, HALF], [1, P]], channel_multiplier=-HEAD_D)
            nc.gpsimd.iota(part_i[:, :], pattern=[[0, 1]], base=0, channel_multiplier=1)
            pool.drain()
            nc.gpsimd.affine_select(out=sel, in_=sel, compare_op=ALU.is_ge, fill=0.0, base=HEAD_D - 1,
                                    pattern=[[-P, HALF], [-1, P]], channel_multiplier=HEAD_D)
            pool.drain().then_inc(consts, 1)
            pass_gathers(pool, layer0, 0)

            pool.wait_ge(a_hid, CHUNKS)
            nc.gpsimd.memset(acc[:, :, :], 0.0)
            nc.gpsimd.memset(den, 0.0)
            pool.drain().then_inc(layer1.acc_zero, 1)
            pool.wait_ge(l_out, 64 * CHUNKS)
            pool.wait_ge(l_tail, 16)
            pool.wait_ge(mode_ready, 1)
            bounded = pool.value_load(mode[0:1, 0:1], min_val=0, max_val=1)
            with pool.If(bounded > 0):
                pass_gathers(pool, layer1, 1)
            with pool.Else():
                with pool.Fori(0, GROUPS // 2) as i:
                    for u in range(2):
                        g = i * 2 + u
                        pool.wait_ge(s_idx[u], 32 * i + 32)
                        pool.sem_inc(passed, 1)
                        for j in range(J):
                            for n, tab in ((u, es_tab), (2 + u, ed_tab)):
                                nc.gpsimd.indirect_dma_start(
                                    score_rows(n)[:, j * HEADS:(j + 1) * HEADS], None, tab,
                                    bass.IndirectOffsetOnAxis(ap=idx[:, n, j:j + 1], axis=0)).then_inc(s_rows[u], 16)
                pool.wait_ge(m_out, 16)
                nc.gpsimd.memset(acc[:, :, :], 0.0)
                nc.gpsimd.memset(den, 0.0)
                pool.drain().then_inc(layer1.acc_zero, 1)
                pass_gathers(pool, layer1, 1)

        @block.tensor
        def _(pe):
            pe.wait_ge(const_in, 16 * 12)
            pe.wait_ge(b_in, 48)
            pe.wait_ge(consts, 2)
            pe.wait_ge(acc_zeroed, 1)
            pe.wait_ge(planned, 1)
            pass_matmuls(pe, layer0, 0)

            def product(w, x, ready, out, done):
                for m in range(HALF):
                    for k in range(HALF):
                        last = pe.matmul(banks[out + m][:, 0:CHUNK], w[:, k, m * P:(m + 1) * P], x[:, k, :],
                                         start=(k == 0), stop=(k == HALF - 1))
                last.then_inc(done, 1)

            pe.wait_ge(layer0.group_done, GROUPS)
            with pe.Fori(0, CHUNKS) as c:
                pe.wait_ge(a_hid, c + 1)
                product(w1, buf_b, None, 0, a_pe1)
                pe.wait_ge(a_act1, c + 1)
                product(w2, buf_c, None, 2, a_pe2)
            pe.wait_ge(wz_ready, 1)
            pe.wait_ge(a_act2, CHUNKS)
            with pe.Fori(0, CHUNKS) as c:
                pe.wait_ge(l_res, c + 1)
                for k in range(HALF):
                    last = pe.matmul(banks[0][:, 0:CHUNK], mean_w[:, :], buf_b[:, k, :], start=(k == 0), stop=(k == 1))
                last.then_inc(l_mean, 1)
                pe.wait_ge(l_sq, c + 1)
                for k in range(HALF):
                    last = pe.matmul(banks[1][:, 0:CHUNK], mean_w[:, :], buf_d[:, k, :], start=(k == 0), stop=(k == 1))
                last.then_inc(l_var, 1)
                pe.wait_ge(l_x, c + 1)
                for s in range(4):
                    pe.wait_ge(l_zc, 4 * c + s - 3) if False else None
                    for k in range(HALF):
                        last = pe.matmul(banks[2 + s][0:SUB, 0:D + 2 * HEADS], buf_d[:, k, s * SUB:(s + 1) * SUB],
                                         wz[:, k, :], start=(k == 0), stop=(k == 1))
                    last.then_inc(l_z, 1)

            pe.wait_ge(top_ready, 1)
            pe.transpose(banks[6][0:1, 0:SUB], es_max[0:SUB, 1, 0:1], ident[0:SUB, 0:SUB]).then_inc(top_turned, 1)
            pe.wait_ge(top_one, 1)
            pe.matmul(banks[7][:, 0:1], ones_row[:, :], choice[:, 0:1], start=True, stop=True).then_inc(top_all, 1)
            pe.wait_ge(mode_ready, 1)
            bounded = pe.value_load(mode[0:1, 0:1], min_val=0, max_val=1)
            with pe.If(bounded > 0):
                pe.wait_ge(layer1.acc_zero, 1)
                pass_matmuls(pe, layer1, 1, fast=True)
            with pe.Else():
                for n in range(2):
                    pe.wait_ge(m_last, n + 1)
                    pe.transpose(banks[0][0:HEADS, 0:P], lasts[:, 0:HEADS], ident[:, :])
                    pe.transpose(banks[0][0:HEADS, P:2 * P], lasts[:, HEADS:2 * HEADS], ident[:, :]).then_inc(m_lastT, 1)
                    pe.wait_ge(m_carry, n + 1)
                    pe.transpose(banks[1][:, 0:HEADS], carry_t[0:HEADS, n:n + P], ident[0:HEADS, 0:HEADS]).then_inc(m_carryT, 1)
                pe.wait_ge(layer1.acc_zero, 2)
                pass_matmuls(pe, layer1, 1)
            pe.wait_ge(layer1.group_done, GROUPS)
            with pe.Fori(0, CHUNKS) as c:
                pe.wait_ge(f_rden, c + 1)
                for k in range(HALF):
                    last = pe.matmul(banks[k][:, 0:CHUNK], head_sel[:, k, :], rstd[0:HEADS, :], start=True, stop=True)
                last.then_inc(f_spread, 1)
                pe.wait_ge(f_sum, c + 1)
                for s in range(4):
                    for k in range(HALF):
                        last = pe.transpose(banks[2 + s][0:SUB, k * P:(k + 1) * P], buf_b[:, k, s * SUB:(s + 1) * SUB],
                                            ident[:, :])
                    last.then_inc(f_turn, 1)


        @block.scalar
        def _(act):
            act.wait_ge(planned, 1)
            pass_act(act, layer0, 0)
            with act.Fori(0, CHUNKS) as c:
                act.wait_ge(a_pe1, c + 1)
                for k in range(HALF):
                    last = act.activation(buf_c[:, k, :], banks[k][:, 0:CHUNK], ACT.Relu, bias=cols[:, 0, k:k + 1])
                last.then_inc(a_act1, 1)
                act.wait_ge(a_pe2, c + 1)
                for k in range(HALF):
                    last = act.activation(node_x[:, k, bass.ds(c * CHUNK, CHUNK)], banks[2 + k][:, 0:CHUNK],
                                          ACT.Identity, bias=cols[:, 1, k:k + 1])
                last.then_inc(a_act2, 1)
            act.wait_ge(bn_var, 1)
            act.activation(bn_tmp[:, :], mv[:, :, 1], ACT.Sqrt, bias=bn_eps[:, :]).then_inc(bn_sqrt, 1)
            act.wait_ge(bn_ready, 1)
            with act.Fori(0, CHUNKS) as c:
                at = bass.ds(c * CHUNK, CHUNK)
                act.wait_ge(l_x, c)
                for k in range(HALF):
                    last = act.activation(buf_c[:, k, :], node_x[:, k, at], ACT.Relu,
                                          bias=bn_shift[:, k:k + 1], scale=bn_scale[:, k:k + 1])
                last.then_inc(l_bn, 1)
                act.wait_ge(l_cen, c + 1)
                act.wait_ge(l_zc, 4 * c)
                act.activation(buf_d, buf_c, ACT.Square).then_inc(l_sq, 1)
                act.wait_ge(l_var, c + 1)
                act.activation(rstd, banks[1][:, 0:CHUNK], ACT.Sqrt, bias=ln_eps[:, :]).then_inc(l_std, 1)
                act.wait_ge(l_out, 64 * c)
                for s in range(4):
                    act.wait_ge(l_z, 4 * c + s + 1)
                    act.copy(z_sb[0:SUB, s, :], banks[2 + s][0:SUB, 0:D + 2 * HEADS]).then_inc(l_zc, 1)
            act.wait_ge(mode_ready, 1)
            bounded = act.value_load(mode[0:1, 0:1], min_val=0, max_val=1)
            with act.If(bounded > 0):
                pass_act(act, layer1, 1, fast=True)
            with act.Else():
                pass_act(act, layer1, 1)
            with act.Fori(0, CHUNKS) as c:
                for s in range(4):
                    act.wait_ge(f_mv, 4 * c + s + 1)
                    act.activation(fin_s[0:SUB, s:s + 1], fin_mv[0:SUB, s, 1:2], ACT.Sqrt,
                                   bias=ln_eps[0:SUB, :]).then_inc(f_std, 1)

        @block.vector
        def _(dve):
            def step(ins=None):
                dve.drain()

            dve.wait_ge(consts, 2)
            dve.tensor_copy(part[:, :], part_i[:, :])
            dve.memset(zero_b[:, :], 0.0)
            dve.memset(ones_row[:, :], 1.0)
            dve.memset(es_max[:, :, :], 0.0)
            dve.tensor_copy(iota[:, :], iota_i[:, :])
            dve.memset(mean_w[:, :], 1.0 / D)
            dve.memset(ones_b[:, :], 1.0)
            dve.memset(ln_eps[:, :], LN_EPS)
            dve.memset(bn_eps[:, :], BN_EPS)
            dve.wait_ge(const_in, 16 * 12)
            dve.tensor_copy(b_part[:, 0, :], b_row[:, :])
            step()
            dve.tensor_tensor(b_rest[:, 0, :], b_row[:, :], b_part[:, 0, :], ALU.subtract)
            step()
            dve.tensor_copy(b_part[:, 1, :], b_rest[:, 0, :])
            step()
            dve.tensor_tensor(b_rest[:, 1, :], b_rest[:, 0, :], b_part[:, 1, :], ALU.subtract)
            step()
            dve.tensor_copy(b_part[:, 2, :], b_rest[:, 1, :])
            dve.drain().then_inc(b_split, 1)
            dve.tensor_scalar(eps1[:, :], eps1[:, :], 1.0, None, ALU.add)
            dve.wait_ge(dst_in, 48)
            dve.tensor_copy(first_f[:, :], firsts[:, 0, :])
            dve.tensor_copy(plan[:, 0, :], firsts[0:1, 0, :])
            step()
            dve.tensor_scalar(node_at[:, :], first_f[:, :], part[:, 0:1], None, ALU.add)
            dve.tensor_tensor(plan[:, 1, :], firsts[0:1, 1, :], firsts[0:1, 0, :], ALU.subtract)
            step()
            dve.tensor_scalar(plan[:, 1, :], plan[:, 1, :], WIN.bit_length() - 1, None, ALU.arith_shift_right)
            step()
            dve.tensor_copy(plan_f[:, 0, :], plan[:, 1, :])
            dve.memset(plan_f[:, 1, :], 1.0)
            step()
            dve.tensor_tensor_scan(plan_f[:, 2, :], plan_f[:, 1, :], plan_f[:, 0, :], 0.0, ALU.mult, ALU.add)
            dve.tensor_scalar(plan[:, 1, :], plan_f[:, 0, :], 1.0, None, ALU.add)
            step()
            dve.tensor_tensor(plan[:, 2, :], plan_f[:, 2, :], plan_f[:, 0, :], ALU.subtract)
            dve.tensor_tensor(dst_off[:, :, :], dst_raw[:, :].rearrange("p (g j) -> p g j", j=J),
                              first_f[:, :].unsqueeze(2).to_broadcast([P, GROUPS, J]), ALU.subtract)
            dve.drain().then_inc(planned, 1)
            dve.memset(acc[:, :, :], 0.0)
            dve.drain().then_inc(acc_zeroed, 1)
            pass_vector(dve, layer0, 0)

            for n in range(2):
                for k in range(HALF):
                    dve.tensor_tensor(buf_c[:, k, 0:D], wz[:, k, 0:D], att[:, n, :], ALU.mult)
                    step()
                    dve.tensor_reduce(wz[:, k, D + n * HEADS:D + (n + 1) * HEADS],
                                      buf_c[:, k, 0:D].rearrange("p (h f) -> p h f", h=HEADS), AX.X, ALU.add)
            dve.drain().then_inc(wz_ready, 1)

            def node_sums(c, at, n):
                dve.wait_ge(chunk_x, 16 * c + 16)
                if not isinstance(c, int) or c > 0:
                    dve.wait_ge(a_pe1, c)
                dve.scalar_tensor_tensor(buf_b, buf_a, eps1[:, 0:1], acc[:, :, at], ALU.mult, ALU.add).then_inc(a_hid, 1)
                dve.wait_ge(a_act2, c + 1)
                for k in range(HALF):
                    dve.bn_stats(stats[:, k, bass.ds(c, 1), :].rearrange("p a s -> p (a s)") if not isinstance(c, int)
                                 else stats[:, k, c, :], node_x[:, k, at][:, 0:n])

            with dve.Fori(0, CHUNKS - 1) as c:
                node_sums(c, bass.ds(c * CHUNK, CHUNK), CHUNK)
            node_sums(CHUNKS - 1, slice((CHUNKS - 1) * CHUNK, CHUNKS * CHUNK), TAIL)
            step()
            for k in range(HALF):
                dve.bn_aggr(mv[:, k, :], stats[:, k, :, :].rearrange("p c s -> p (c s)"))
            dve.drain().then_inc(bn_var, 1)
            dve.wait_ge(bn_sqrt, 1)
            dve.reciprocal(bn_shift[:, :], bn_tmp[:, :])
            step()
            dve.tensor_tensor(bn_scale[:, :], bn_shift[:, :], cols[:, 2, :], ALU.mult)
            step()
            dve.tensor_tensor(bn_tmp[:, :], bn_scale[:, :], mv[:, :, 0], ALU.mult)
            step()
            dve.tensor_tensor(bn_shift[:, :], cols[:, 3, :], bn_tmp[:, :], ALU.subtract)
            dve.drain().then_inc(bn_ready, 1)

            with dve.Fori(0, CHUNKS) as c:
                at = bass.ds(c * CHUNK, CHUNK)
                dve.wait_ge(chunk_y, 16 * c + 16)
                dve.wait_ge(l_bn, c + 1)
                dve.tensor_tensor(buf_b, buf_a, buf_c, ALU.add).then_inc(l_res, 1)
                dve.wait_ge(l_mean, c + 1)
                for k in range(HALF):
                    last = dve.tensor_tensor(buf_c[:, k, :], buf_b[:, k, :], banks[0][:, 0:CHUNK], ALU.subtract)
                last.then_inc(l_cen, 1)
                dve.wait_ge(l_std, c + 1)
                dve.reciprocal(rstd, rstd)
                step()
                dve.tensor_tensor(buf_d, buf_c, rstd.unsqueeze(1).to_broadcast([P, HALF, CHUNK]), ALU.mult)
                step()
                dve.tensor_copy(node_x[:, :, at], buf_d)
                dve.drain().then_inc(l_x, 1)
                dve.wait_ge(l_zc, 4 * c + 4)
                dve.wait_ge(l_out, 64 * c)
                es, ed = (z_sb[0:SUB, :, lo:lo + HEADS] for lo in (D, D + HEADS))
                rest = [ed, ed_rest[0:SUB, 0], ed_rest[0:SUB, 1]]
                for q in range(PARTS):
                    dve.tensor_copy(ed_split[0:SUB, :, q, :], rest[q])
                    step()
                    if q < PARTS - 1:
                        dve.tensor_tensor(rest[q + 1], rest[q], ed_split[0:SUB, :, q, :], ALU.subtract)
                        step()
                four = lambda n: es_max[0:SUB, n, :].rearrange("p (s h) -> p s h", s=4)
                dve.scalar_tensor_tensor(four(1), es, -1.0, es, ALU.mult, ALU.max)
                step()
                dve.tensor_tensor(four(0), four(0), four(1), ALU.max)
                dve.drain().then_inc(l_split, 1)

            dve.tensor_reduce(es_max[0:SUB, 1, 0:1], es_max[0:SUB, 0, :], AX.X, ALU.max).then_inc(top_ready, 1)
            dve.wait_ge(top_turned, 1)
            dve.tensor_reduce(choice[:, 0:1], banks[6][0:1, 0:SUB], AX.X, ALU.max)
            dve.tensor_reduce(choice[:, 1:2], plan[:, 1, :], AX.X, ALU.max)
            dve.drain().then_inc(top_one, 1)
            dve.wait_ge(top_all, 1)
            dve.tensor_copy(es_top[:, :], banks[7][:, 0:1])
            dve.tensor_scalar(choice[:, 2:3], choice[:, 0:1], ES_LIMIT, None, ALU.is_le)
            dve.tensor_scalar(choice[:, 3:4], choice[:, 1:2], 1.0, None, ALU.is_le)
            step()
            dve.tensor_tensor(mode[:, :], choice[:, 2:3], choice[:, 3:4], ALU.mult)
            dve.drain().then_inc(mode_ready, 1)

            bounded = dve.value_load(mode[0:1, 0:1], min_val=0, max_val=1)
            with dve.If(bounded > 0):
                dve.wait_ge(layer1.acc_zero, 1)
                pass_vector(dve, layer1, 1, fast=True)
            with dve.Else():
                with dve.Fori(0, GROUPS // 2) as i:
                    for u in range(2):
                        g = i * 2 + u
                        a, b = score_rows(u), score_rows(2 + u)
                        e = expo[:, u, :]
                        dve.wait_ge(s_stored[u], 16 * i)
                        dve.wait_ge(s_rows[u], 2 * 16 * J * (i + 1))
                        dve.tensor_tensor(a, a, b, ALU.add)
                        step()
                        dve.scalar_tensor_tensor(b, a, SLOPE, a, ALU.mult, ALU.max)
                        step()
                        dve.tensor_scalar(a, b, 0.0, NEG, ALU.is_equal, ALU.mult)
                        step()
                        dve.tensor_tensor(e, a, b, ALU.add).then_inc(s_score, 1)

                dve.wait_ge(m_in, 64)
                before, here, after = (line_dst(n) for n in range(3))
                dve.tensor_tensor(pen_in, here, before, ALU.not_equal)
                dve.tensor_tensor(pen_out, here, after, ALU.not_equal)
                step()
                dve.tensor_scalar(pen_in, pen_in, FAR, None, ALU.mult)
                dve.tensor_scalar(pen_out, pen_out, FAR, None, ALU.mult)
                dve.memset(carry_t[0:HEADS, :], FAR)
                step()
                e = acc_line(0).rearrange("p (n h) -> p n h", h=HEADS)
                f = acc_line(1).rearrange("p (n h) -> p n h", h=HEADS)
                for n in range(2):
                    pen, data, way = ((pen_in, e, slice(None)), (pen_out, f, slice(None, None, -1)))[n]
                    end = (LINE - 1, 0)[n]
                    for h in range(HEADS):
                        dve.tensor_tensor_scan(run_max[:, way], pen[:, way], data[:, way, h], FAR, ALU.add, ALU.max)
                        step()
                        dve.tensor_copy(lasts[:, h:h + 1], run_max[:, end:end + 1])
                        dve.tensor_reduce(lasts[:, HEADS + h:HEADS + h + 1], pen, AX.X, ALU.min)
                        step()
                    dve.drain().then_inc(m_last, 1)
                    dve.wait_ge(m_lastT, n + 1)
                    dve.tensor_copy(carry_sb[0:HEADS, :], banks[0][0:HEADS, 0:2 * P])
                    step()
                    dve.tensor_tensor_scan(carry_t[0:HEADS, 1:P + 1][:, way], carry_sb[0:HEADS, P:2 * P][:, way],
                                           carry_sb[0:HEADS, 0:P][:, way], FAR, ALU.add, ALU.max)
                    step()
                    if n == 1:
                        dve.tensor_copy(carry_sb[0:HEADS, 0:P], carry_t[0:HEADS, 1:P + 1])
                        step()
                        dve.memset(carry_t[0:HEADS, P:P + 1], FAR)
                        dve.tensor_copy(carry_t[0:HEADS, 1:P], carry_sb[0:HEADS, 1:P])
                        step()
                    dve.drain().then_inc(m_carry, 1)
                    dve.wait_ge(m_carryT, n + 1)
                    dve.tensor_copy(carry[:, 0:HEADS], banks[1][:, 0:HEADS])
                    step()
                    for h in range(HEADS):
                        out = f[:, :, h] if n == 0 else run_max
                        dve.tensor_tensor_scan(out[:, way], pen[:, way], data[:, way, h], carry[:, h:h + 1],
                                               ALU.add, ALU.max)
                        step()
                        if n == 1:
                            dve.tensor_tensor(e[:, :, h], e[:, :, h], run_max, ALU.subtract)
                            step()
                dve.tensor_scalar(acc_line(0), acc_line(0), FLOOR, None, ALU.max).then_inc(m_done, 1)
                dve.wait_ge(layer1.acc_zero, 2)
                pass_vector(dve, layer1, 1)

            dve.drain()
            with dve.Fori(0, CHUNKS) as c:
                at = bass.ds(c * CHUNK, CHUNK)
                dve.wait_ge(f_spread, c)
                dve.tensor_scalar(rstd[0:HEADS, :], den[:, at], 0.0, None, ALU.is_le)
                step()
                dve.tensor_tensor(rstd[0:HEADS, :], rstd[0:HEADS, :], den[:, at], ALU.add)
                step()
                dve.reciprocal(rstd[0:HEADS, :], rstd[0:HEADS, :]).then_inc(f_rden, 1)
                dve.wait_ge(f_spread, c + 1)
                dve.wait_ge(f_turn, 4 * c)
                for k in range(HALF):
                    dve.tensor_tensor(buf_b[:, k, :], acc[:, k, at], banks[k][:, 0:CHUNK], ALU.mult)
                step()
                dve.tensor_tensor(buf_b, buf_b, node_x[:, :, at], ALU.add).then_inc(f_sum, 1)
                dve.wait_ge(f_out, 16 * c)
                for s in range(4):
                    x = banks[2 + s][0:SUB, 0:D]
                    dve.wait_ge(f_turn, 4 * c + s + 1)
                    dve.bn_stats(fin_stats[0:SUB, s, :], x)
                    step()
                    dve.bn_aggr(fin_mv[0:SUB, s, :], fin_stats[0:SUB, s, :])
                    dve.drain().then_inc(f_mv, 1)
                for s in range(4):
                    x = banks[2 + s][0:SUB, 0:D]
                    dve.wait_ge(f_std, 4 * c + s + 1)
                    dve.reciprocal(fin_r[0:SUB, s:s + 1], fin_s[0:SUB, s:s + 1])
                    step()
                    dve.tensor_scalar(fin[0:SUB, s, :], x, fin_mv[0:SUB, s, 0:1], fin_r[0:SUB, s:s + 1],
                                      ALU.subtract, ALU.mult).then_inc(f_nrm, 1)


def kernel(x, src, dst, edge_attr_128, L0_gnn_W_edge, L0_gnn_b_edge, L0_gnn_W1, L0_gnn_b1, L0_gnn_W2, L0_gnn_b2,
           L0_gnn_eps, L0_gnn_gamma, L0_gnn_beta, L1_gnn_W, L1_gnn_att):
    import numpy as np
    import concourse.bacc as bacc
    from concourse.bass_utils import run_bass_kernel_spmd

    x, edge = np.asarray(x), np.asarray(edge_attr_128)
    pad = EPAD - EDGES
    src_p = np.concatenate([np.asarray(src), np.zeros(pad, np.int32)])
    dst_p = np.concatenate([np.asarray(dst), np.full(pad, NODES, np.int32)])
    edge_p = np.concatenate([edge, np.zeros((pad, EDGE_D), edge.dtype)])
    x_t = np.zeros((D, NPAD), x.dtype)
    x_t[:, :NODES] = x.T
    by_half = lambda w: np.ascontiguousarray(np.asarray(w).reshape(HALF, P, -1).transpose(1, 0, 2))
    by_col = lambda v: np.ascontiguousarray(np.asarray(v).reshape(HALF, P).T)
    att = np.asarray(L1_gnn_att)
    end = np.full(1, -1, np.int32)
    arrays = {
        "x": x,
        "src_idx": src_p.reshape(GROUPS, P, J),
        "dst_idx": dst_p.reshape(GROUPS, P, J),
        "dst_pm": dst_p.reshape(GROUPS, P, J).transpose(1, 0, 2).reshape(P, GROUPS * J),
        "dst_ext": np.concatenate([end, dst_p, end]).reshape(1, EPAD + 2),
        "dst_jp": dst_p.reshape(GROUPS, P, J).transpose(0, 2, 1).reshape(GROUPS, 1, GROUP),
        "first": dst_p[::GROUP].reshape(1, GROUPS),
        "last": dst_p[GROUP - 1::GROUP].reshape(1, GROUPS),
        "edge_t": edge_p.reshape(GROUPS, P, J, EDGE_D).transpose(0, 3, 2, 1).reshape(GROUPS, EDGE_D, GROUP),
        "x_t": by_half(x_t),
        "w_edge": np.asarray(L0_gnn_W_edge),
        "b_edge": np.asarray(L0_gnn_b_edge).reshape(1, D),
        "w1": by_half(L0_gnn_W1), "w2": by_half(L0_gnn_W2),
        "b1": by_col(L0_gnn_b1), "b2": by_col(L0_gnn_b2),
        "gamma": by_col(L0_gnn_gamma), "beta": by_col(L0_gnn_beta),
        "eps": np.asarray(L0_gnn_eps).reshape(1, 1),
        "wz": by_half(np.asarray(L1_gnn_W).transpose(1, 0, 2).reshape(D, D)),
        "att_src": att[:, :HEAD_D].reshape(1, D), "att_dst": att[:, HEAD_D:].reshape(1, D),
    }
    nc = bacc.Bacc("TRN2", target_bir_lowering=False, num_devices=1)
    feeds, t = {}, {}
    for name, a in arrays.items():
        a = np.ascontiguousarray(a)
        feeds[f"in_{name}"] = a
        t[name] = nc.dram_tensor(f"in_{name}", a.shape, mybir.dt.from_np(a.dtype), kind="ExternalInput").ap()
    t["out"] = nc.dram_tensor("out_0", (NODES, D), F32, kind="ExternalOutput").ap()
    build(nc, t)
    r = run_bass_kernel_spmd(nc, [feeds], core_ids=[0])
    return r.results[0]["out_0"]
```

```python
from contextlib import ExitStack

import concourse.bass as bass
from concourse import mybir

ALU = mybir.AluOpType
ACT = mybir.ActivationFunctionType
AX = mybir.AxisListType
F32 = mybir.dt.float32
BF16 = mybir.dt.bfloat16
I32 = mybir.dt.int32

P = 128
NODES = 6250
EDGES = 200000
D = 256
HALF = D // P
EDGE_D = 128
HEADS = 4
HEAD_D = D // HEADS
J = 8
GROUP = P * J
GROUPS = -(-EDGES // GROUP)
EPAD = GROUPS * GROUP
RING = 4
ROUNDS = GROUPS // RING
PAIRS = J // 2
WIN = 128
ROW = D + HEADS
CHUNK = 448
CHUNKS = -(-NODES // CHUNK)
NPAD = CHUNK * CHUNKS
TAIL = NODES - CHUNK * (CHUNKS - 1)
TILES = 4
SUB = CHUNK // TILES
STEPS = CHUNKS // 2
ACC_W = NPAD + WIN
LINE = EPAD // P
BN_EPS = 1e-5
LN_EPS = 1e-5
SLOPE = 0.01
NEG = -1000.0
FAR = -1e30
TINY = 1e-37
FLOOR = -80.0
ES_LIMIT = 19.0
NEG_NEAR = -40.0
PARTS = 3
WEIGHT_LOADS = 9


def build(nc, t):
    with ExitStack() as ctx:
        def sb(name, shape, dt=F32):
            return ctx.enter_context(nc.sbuf_tensor(name, shape, dt))

        def sem(name):
            return ctx.enter_context(nc.semaphore(name))

        def dram(name, shape, dt=F32):
            return nc.dram_tensor(name, shape, dt).ap()

        z_tab = dram("z_tab", (NPAD, ROW))
        es_tab = dram("es_tab", (NPAD, HEADS))
        ed_tab = dram("ed_tab", (NPAD, HEADS))
        ed_parts = dram("ed_parts", (NPAD + WIN, PARTS * HEADS), BF16)
        score_tab = dram("score_tab", (GROUPS, P, J * HEADS))
        expo_tab = dram("expo_tab", (GROUPS, P, J * HEADS))

        acc = sb("acc", [P, HALF, ACC_W])
        node_x = sb("node_x", [P, HALF, NPAD])
        rows = sb("rows", [P, RING, J, ROW])
        edge_room = sb("edge_room", [P, ACC_W])
        edge_in = edge_room[:, 0:RING * GROUP].rearrange("p (r n) -> p r n", r=RING)
        den = edge_room[0:HEADS, :]
        onehot = sb("onehot", [P, 3, J, WIN])
        idx = sb("idx", [P, RING, J], I32)
        dst_off = sb("dst_off", [P, GROUPS, J])
        off_here = sb("off_here", [P, J])
        first_f = sb("first_f", [P, GROUPS])
        node_at = sb("node_at", [P, GROUPS + 1])
        dst_t = sb("dst_t", [P, 2, GROUP], I32)
        hot_t = sb("hot_t", [P, GROUP], BF16)
        ed_win = sb("ed_win", [P, RING, PARTS * HEADS], BF16)
        score = sb("score", [P, 3, J * HEADS])
        lrelu = sb("lrelu", [P, 2, J * HEADS])
        es_max = sb("es_max", [P, 1])
        es_top = sb("es_top", [P, 1])
        choice = sb("choice", [1, 4])
        mode = sb("mode", [1, 1], I32)
        zero_b = sb("zero_b", [P, PARTS * HEADS], BF16)
        part_i = sb("part_i", [P, 1], I32)
        part = sb("part", [P, 1])
        ones_row = sb("ones_row", [1, P])
        plan = sb("plan", [1, 3, GROUPS], I32)
        agg_sb = sb("agg_sb", [WIN, ROW])
        expo = sb("expo", [P, RING, J * HEADS])
        iota_i = sb("iota_i", [P, WIN], I32)
        iota = sb("iota", [P, WIN])
        ident = sb("ident", [P, P])
        mean_w = sb("mean_w", [P, P])
        b_edge = sb("b_edge", [P, D])
        w1x = sb("w1x", [P, HALF, D])
        weights = sb("weights", [P, 5 * CHUNK])
        cols = sb("cols", [P, 4, HALF])
        eps1 = sb("eps1", [P, 1])
        ln_eps = sb("ln_eps", [P, 1])
        bn_eps = sb("bn_eps", [P, 1])
        stats = sb("stats", [P, HALF, CHUNKS, 6])
        mv = sb("mv", [P, HALF, 2])
        bn_scale = sb("bn_scale", [P, HALF])
        bn_shift = sb("bn_shift", [P, HALF])
        bn_tmp = sb("bn_tmp", [P, HALF])
        counts = sb("counts", [P, 1])
        is_early = sb("is_early", [1, CHUNKS + 1])
        single = sb("single", [1, 1], I32)
        zero_f = sb("zero_f", [P, 1])
        node_ends = sb("node_ends", [1, CHUNKS + 2], I32)
        fin_stats = sb("fin_stats", [P, TILES, 6])
        fin_mv = sb("fin_mv", [P, TILES, 2])
        fin_s = sb("fin_s", [P, TILES])
        fin_r = sb("fin_r", [P, TILES])
        fin_m = sb("fin_m", [P, TILES])
        fin_den = sb("fin_den", [P, TILES, HEADS])
        table_in = sb("table_in", [P, 2])

        early = node_x[:, :, :].rearrange("p k n -> p (k n)")
        dst_raw = early[:, 12 * D:12 * D + GROUPS * J].bitcast(I32)
        firsts = early[:, 20 * D:20 * D + 2 * GROUPS].bitcast(I32).rearrange("p (a n) -> p a n", a=2)
        is_before = early[:, 32 * D:32 * D + GROUPS]
        att = hot_t[:, :].bitcast(F32).rearrange("p (a n) -> p a n", a=2)
        plan_f = early[0:1, 24 * D:24 * D + 3 * GROUPS].rearrange("p (a n) -> p a n", a=3)

        spare = rows[:, :, :, :].rearrange("p r j c -> p (r j c)")

        def halves(ap):
            return ap.rearrange("p (k n) -> p k n", k=HALF)

        def carve(room):
            used = [0]

            def take(*shape):
                size = 1
                for n in shape:
                    size *= n
                ap = room[:, used[0]:used[0] + size]
                used[0] += size
                names = "abc"[:len(shape)]
                sizes = dict(zip(names, shape))
                return ap.rearrange(f"p ({' '.join(names)}) -> p {' '.join(names)}", **sizes) if len(shape) > 1 else ap
            return take

        take = carve(spare)
        buf_r, buf_c, buf_n = ([take(HALF, CHUNK) for b in range(2)] for n in range(3))
        x_in = [halves(dst_t[:, b, 0:HALF * CHUNK].bitcast(F32)) for b in range(2)]
        take = carve(edge_room)
        wz_tmp = take(2 * HALF, D)
        take = carve(edge_room)
        z_sb = [take(TILES, ROW) for b in range(2)]
        rstd = [take(CHUNK) for b in range(2)]
        score_all = take(CHUNKS * TILES, 2 * HEADS)
        es_abs = take(CHUNKS * TILES, HEADS)
        ed_rest = take(2, TILES, HEADS)
        ed_split = take(CHUNKS * TILES, PARTS * HEADS // 2).rearrange("p s c -> p (s c)").bitcast(BF16).rearrange(
            "p (s q h) -> p s q h", q=PARTS, h=HEADS)
        take = carve(weights[:, :])
        w_edge = take(D)
        w1, w2 = (take(HALF, D) for n in range(2))
        wz = take(HALF, D + 2 * HEADS)
        take = carve(weights[:, :])
        sums_c, x_c = (take(HALF, CHUNK) for n in range(2))
        den_c = take(CHUNK)[0:HEADS, :]
        out_c = onehot[:, 2, :, :].rearrange("p j n -> p (j n)").rearrange("p (s c) -> p s c", s=TILES)

        flat = acc[:, :, :].rearrange("p k n -> p (k n)")

        def acc_line(n):
            return flat[:, n * LINE * HEADS:(n + 1) * LINE * HEADS]

        def line_dst(n):
            return spare[:, n * LINE:(n + 1) * LINE].bitcast(I32)

        pen_in, pen_out = (spare[:, n * LINE:(n + 1) * LINE] for n in (3, 4))
        edge_flat = edge_room
        run_max = edge_flat[:, 0:LINE]
        lasts = edge_flat[:, LINE:LINE + 16]
        carry_t = edge_flat[:, LINE + 16:LINE + 16 + 2 * P + 2]
        carry = edge_flat[:, LINE + 300:LINE + 300 + 2 * HEADS]
        carry_sb = edge_flat[:, LINE + 320:LINE + 320 + 2 * P]

        def score_rows(n):
            return spare[:, n * J * HEADS:(n + 1) * J * HEADS]

        psum = ctx.enter_context(nc.psum_tensor("psum", [P, 8, 512], F32))
        banks = [psum[:, n, :] for n in range(8)]
        agg_ps, turn_ps = banks[4], banks[5]

        const_in = sem("const_in")
        edge_w_in = sem("edge_w_in")
        counted, ends_ready = sem("counted"), sem("ends_ready")
        zero_ready = sem("zero_ready")
        dst_in = sem("dst_in")
        passed = sem("passed")
        consts = sem("consts")
        acc_zeroed = sem("acc_zeroed")
        planned = sem("planned")

        class Layer:
            def __init__(self, n):
                s = lambda name: sem(f"{name}{n}")
                self.idx_in = [s(f"idx_in_{u}_") for u in range(RING)]
                self.rows_in = [s(f"rows_in_{u}_") for u in range(RING)]
                self.edge_in = [s(f"edge_in_{u}_") for u in range(RING)]
                self.edge_done, self.summed, self.msg_ready = s("edge_done"), s("summed"), s("msg_ready")
                self.onehot_ready, self.agg_ready, self.agg_copied = s("onehot"), s("agg"), s("aggc")
                self.turned, self.group_done = s("turned"), s("group_done")
                self.x_onehot, self.x_agg, self.x_copied = s("x_onehot"), s("x_agg"), s("x_copied")
                self.x_turned, self.x_added = s("x_turned"), s("x_added")
                self.acc_zero = s("acc_zero")
                self.spread_hot, self.scored = s("spread_hot"), s("scored")
                self.ed_in = [s(f"ed_in_{u}_") for u in range(RING)] if n else []
                self.dst_in = [s(f"dst_in_{u}_") for u in range(2)] if n else []

        layer0, layer1 = Layer(0), Layer(1)

        def two(name):
            return [sem(f"{name}{b}_") for b in range(2)]

        a_in, a_pe1, a_act1, a_pe2, a_act2 = (sem(f"a_{x}") for x in ("in", "pe1", "act1", "pe2", "act2"))
        w1x_ready = sem("w1x_ready")
        bn_var, bn_sqrt, bn_ready = sem("bn_var"), sem("bn_sqrt"), sem("bn_ready")
        l_in, l_res, l_var, l_x, l_keep, l_z, l_zc, l_zout, l_eout = (
            two(f"l_{x}") for x in ("in", "res", "var", "x", "keep", "z", "zc", "zout", "eout"))
        l_bn, l_mean, l_cen, l_sq, l_std, l_split = (sem(f"l_{x}") for x in ("bn", "mean", "cen", "sq", "std", "split"))
        wz_ready = sem("wz_ready")
        l_tail, top_ready, top_turned, top_one, top_all, mode_ready = (
            sem(f"l_{x}") for x in ("tail", "top", "topT", "top1", "topA", "mode"))
        tabs_out = sem("tabs_out")
        s_idx = [sem(f"s_idx{u}") for u in range(2)]
        s_rows = [sem(f"s_rows{u}") for u in range(2)]
        s_score = sem("s_score")
        s_stored = [sem(f"s_stored{u}") for u in range(2)]
        m_in = sem("m_in")
        m_pen = sem("m_pen")
        m_last, m_lastT, m_carry, m_carryT = (sem(f"m_{x}") for x in ("last", "lastT", "carry", "carryT"))
        m_done = sem("m_done")
        m_out = sem("m_out")
        f_copied, f_den, f_turn, f_mv, f_std, f_r, f_nrm, f_out = (
            sem(f"f_{x}") for x in ("copied", "den", "turn", "mv", "std", "r", "nrm", "out"))

        block = ctx.enter_context(nc.Block())


        def rounds(eng, body, finish_nodes=None):
            def until(lo, hi):
                with eng.Fori(lo, hi) as n:
                    for u in range(RING):
                        body(n + 1, u, (n + 1) * RING + u)

            def end(n):
                return eng.value_load(node_ends[0:1, bass.ds(n, 1)], min_val=0, max_val=ROUNDS - 1)

            for u in range(RING):
                body(0, u, u)
            if finish_nodes is None:
                return until(0, ROUNDS - 1)
            chunks = eng.value_load(node_ends[0:1, CHUNKS + 1:CHUNKS + 2], min_val=0, max_val=CHUNKS - 1)
            with eng.If(chunks > 0):
                with eng.Fori(0, chunks) as c:
                    lo, hi = end(c), end(c + 1)
                    with eng.If(hi > lo):
                        until(lo, hi)
                    finish_nodes(c, hi * RING + RING - 1)
            lo = end(chunks)
            with eng.If(lo < ROUNDS - 1):
                until(lo, ROUNDS - 1)
            return chunks

        def last_nodes(eng, finish_nodes, c0):
            with eng.If(c0 < CHUNKS - 1):
                with eng.Fori(c0, CHUNKS - 1) as c:
                    finish_nodes(c, GROUPS)
            finish_nodes(CHUNKS - 1, GROUPS)

        def first_round(i):
            return isinstance(i, int) and i == 0

        def pass_loads(sp, L, layer, fast=False):
            def load_ends(i, u, g):
                of_padding = isinstance(g, int) and g == GROUPS
                base = 0 if of_padding else sp.value_load(plan[0:1, 0, bass.ds(g, 1)], min_val=0, max_val=NODES)
                if not (first_round(i) and g < 2):
                    sp.wait_ge(L.spread_hot, g - 1)
                    sp.sem_inc(passed, 1)
                sp.dma_start(dst_t[:, u % 2, :], t["dst_jp"][g].to_broadcast([P, GROUP])).then_inc(L.dst_in[u % 2], 16)
                if not first_round(i):
                    sp.wait_ge(L.edge_done, g - RING + 1)
                sp.sem_inc(passed, 1)
                sp.dma_start(ed_win[:, u, :], ed_parts[bass.ds(base, WIN), :]).then_inc(L.ed_in[u], 16)

            def load_nodes(c, done):
                sp.wait_ge(a_pe1, HALF * c)
                sp.sem_inc(passed, 1)
                sp.dma_start(x_in[0], t["x_t"][:, :, bass.ds(c * CHUNK, CHUNK)]).then_inc(a_in, 16)

            def body(i, u, g):
                if layer == 0 and first_round(i):
                    return
                if not first_round(i):
                    sp.wait_ge(L.rows_in[u], 16 * J * i)
                sp.dma_start(idx[:, u, :], t["src_idx"][g]).then_inc(L.idx_in[u], 16)
                if layer == 0:
                    sp.wait_ge(L.edge_done, PAIRS * (g - RING + 1))
                    sp.dma_start(edge_in[:, u, :], t["edge_t"][g]).then_inc(L.edge_in[u], 16)
                elif fast:
                    load_ends(i, u, g)
                else:
                    if not first_round(i):
                        sp.wait_ge(L.group_done, g - RING + 1)
                    sp.dma_start(expo[:, u, :], expo_tab[g]).then_inc(L.edge_in[u], 16)
            c0 = rounds(sp, body, load_nodes if fast and layer == 0 else None)
            if layer == 0:
                last_nodes(sp, load_nodes, c0 if fast else 0)
            if fast and layer == 1:
                load_ends(ROUNDS, 0, GROUPS)

        def pass_gathers(pool, L, layer):
            table, width = (t["x"], D) if layer == 0 else (z_tab, ROW)

            def body(i, u, g):
                if not first_round(i):
                    pool.wait_ge(L.group_done, g - RING + 1)
                    pool.sem_inc(passed, 1)
                pool.wait_ge(L.idx_in[u], 16 * i + 16)
                if not first_round(i):
                    pool.sem_inc(passed, 1)
                for j in range(J):
                    nc.gpsimd.indirect_dma_start(
                        rows[:, u, j, 0:width], None, table,
                        bass.IndirectOffsetOnAxis(ap=idx[:, u, j:j + 1], axis=0)).then_inc(L.rows_in[u], 16)
            rounds(pool, body)

        def turn(pe, L, dst_sem):
            pe.sem_inc(passed, 1)
            for k in range(HALF):
                last = pe.transpose(turn_ps[:, k * WIN:(k + 1) * WIN], agg_sb[:, k * P:(k + 1) * P],
                                    ident[:, :])
            if L is layer1:
                last = pe.transpose(turn_ps[0:HEADS, HALF * WIN:(HALF + 1) * WIN], agg_sb[:, D:ROW],
                                    ident[:, :])
            last.then_inc(dst_sem, 1)

        def mlp_pe(pe, group_done):
            def finish_nodes(c, done):
                pe.wait_ge(w1x_ready, 1)
                pe.wait_ge(a_in, 16 * c + 16)
                pe.wait_ge(a_act2, c)
                for m in range(HALF):
                    for k in range(HALF):
                        pe.matmul(banks[6 + m][:, 0:CHUNK], w1x[:, k, m * P:(m + 1) * P], x_in[0][:, k, :],
                                  start=(k == 0), stop=False)
                pe.wait_ge(group_done, done)
                for m in range(HALF):
                    for k in range(HALF):
                        last = pe.matmul(banks[6 + m][:, 0:CHUNK], w1[:, k, m * P:(m + 1) * P],
                                         acc[:, k, bass.ds(c * CHUNK, CHUNK)], start=False, stop=(k == HALF - 1))
                    last.then_inc(a_pe1, 1)
                for m in range(HALF):
                    for k in range(HALF):
                        if m == 0:
                            pe.wait_ge(a_act1, 2 * c + k + 1)
                        last = pe.matmul(banks[6 + m][:, 0:CHUNK], w2[:, k, m * P:(m + 1) * P], x_in[1][:, k, :],
                                         start=(k == 0), stop=(k == HALF - 1))
                last.then_inc(a_pe2, 1)
            return finish_nodes

        def mlp_act(act):
            def finish_nodes(c, done):
                act.wait_ge(const_in, 16 * WEIGHT_LOADS)
                for k in range(HALF):
                    act.wait_ge(a_pe1, 2 * c + k + 1)
                    act.activation(x_in[1][:, k, :], banks[6 + k][:, 0:CHUNK], ACT.Relu,
                                   bias=cols[:, 0, k:k + 1]).then_inc(a_act1, 1)
                act.wait_ge(a_pe2, c + 1)
                for k in range(HALF):
                    ins = act.activation(node_x[:, k, bass.ds(c * CHUNK, CHUNK)], banks[6 + k][:, 0:CHUNK],
                                         ACT.Identity, bias=cols[:, 1, k:k + 1])
                ins.then_inc(a_act2, 1)
            return finish_nodes

        def mlp_dve(dve, variant):
            prev = dve.alloc_register(f"prev_chunk{variant}")

            def statistics(c, n):
                for k in range(HALF):
                    dve.bn_stats(stats[:, k, bass.ds(c, 1), :].rearrange("p a s -> p (a s)"),
                                 node_x[:, k, bass.ds(c * CHUNK, n)])

            def finish_nodes(c, done):
                if isinstance(c, int):
                    dve.wait_ge(a_act2, c)
                    statistics(c - 1, CHUNK)
                    dve.wait_ge(a_act2, c + 1)
                    statistics(c, TAIL)
                else:
                    with dve.If(c > 0):
                        dve.wait_ge(a_act2, c)
                        dve.sem_inc(passed, 1)
                        dve.reg_mov(prev, c - 1)
                        statistics(dve.snap(prev, min_val=0, max_val=CHUNKS - 2), CHUNK)
            return finish_nodes

        def finish_nodes_pe(pe):
            def turn_tiles(x, out):
                for s in range(TILES):
                    for k in range(HALF):
                        last = pe.transpose(psum[0:SUB, out + s // 2, (s % 2) * D + k * P:(s % 2) * D + (k + 1) * P],
                                            x[:, k, s * SUB:(s + 1) * SUB], ident[:, :])
                    if out == 2 and s % 2 == 1:
                        last.then_inc(f_turn, 1)

            def finish_nodes(c, done):
                pe.wait_ge(f_copied, 3 * c + 1)
                pe.wait_ge(f_mv, c)
                turn_tiles(x_c, 6)
                pe.wait_ge(f_copied, 3 * c + 2)
                pe.sem_inc(passed, 1)
                for s in range(TILES):
                    last = pe.transpose(turn_ps[0:SUB, s * HEADS:(s + 1) * HEADS], den_c[:, s * SUB:(s + 1) * SUB],
                                        ident[0:HEADS, 0:HEADS])
                last.then_inc(f_den, 1)
                pe.wait_ge(f_copied, 3 * c + 3)
                turn_tiles(sums_c, 2)
                pe.wait_ge(f_den, 2 * c + 2)
            return finish_nodes

        def finish_nodes_act(act, group_done):
            def finish_nodes(c, done):
                at = bass.ds(c * CHUNK, CHUNK)
                act.wait_ge(f_turn, 2 * c)
                act.copy(x_c, node_x[:, :, at]).then_inc(f_copied, 1)
                act.wait_ge(group_done, done)
                act.copy(den_c, den[:, at]).then_inc(f_copied, 1)
                act.copy(sums_c, acc[:, :, at]).then_inc(f_copied, 1)
                act.activation(table_in[:, 0:1], ln_eps[:, :], ACT.Sqrt)
                act.wait_ge(f_mv, c + 1)
                act.activation(fin_s[0:SUB, :], fin_mv[0:SUB, :, 1], ACT.Sqrt, bias=ln_eps[0:SUB, :]).then_inc(f_std, 1)
                act.wait_ge(f_r, c + 1)
                for s in range(TILES):
                    ins = act.activation(out_c[0:SUB, s, :], out_c[0:SUB, s, :], ACT.Identity,
                                         bias=fin_m[0:SUB, s:s + 1], scale=fin_r[0:SUB, s:s + 1])
                ins.then_inc(f_nrm, 1)
                act.activation(table_in[:, 1:2], ln_eps[:, :], ACT.Exp)
                act.wait_ge(f_nrm, c + 1)
                act.sem_inc(passed, 1)
                rest = isinstance(c, int) and TAIL % SUB
                whole = TAIL // SUB if rest else TILES
                act.dma_start(t["out"][bass.ds(c * CHUNK, whole * SUB), :].rearrange("(s p) c -> p s c", s=whole),
                              out_c[0:SUB, 0:whole, :]).then_inc(f_out, 16)
                if rest:
                    act.dma_start(t["out"][NODES - rest:NODES, :], out_c[0:rest, whole, :]).then_inc(f_out, 16)
            return finish_nodes

        def finish_nodes_dve(dve):
            def finish_nodes(c, done):
                dve.wait_ge(f_den, 2 * c + 1)
                dve.tensor_scalar(fin_den[0:SUB], turn_ps[0:SUB, 0:TILES * HEADS].rearrange("p (s h) -> p s h", s=TILES),
                                  TINY, None, ALU.max)
                dve.drain()
                dve.reciprocal(fin_den[0:SUB], fin_den[0:SUB])
                dve.drain().then_inc(f_den, 1)
                dve.wait_ge(f_out, 16 * c)
                pair = lambda ap, h: ap[:, 2 * h:2 * h + 2]
                for h in range(2):
                    dve.wait_ge(f_turn, 2 * c + h + 1)
                    dve.tensor_tensor(pair(out_c[0:SUB], h).rearrange("p s (h f) -> p (s h) f", h=HEADS),
                                      psum[0:SUB, 2 + h, :].rearrange("p (s f) -> p s f", f=HEAD_D),
                                      pair(fin_den[0:SUB], h).rearrange("p s h -> p (s h)").unsqueeze(2).to_broadcast(
                                          [SUB, 2 * HEADS, HEAD_D]), ALU.mult)
                dve.drain()
                dve.tensor_tensor(out_c[0:SUB], out_c[0:SUB],
                                  psum[0:SUB, 6:8, :].rearrange("p b (s c) -> p (b s) c", s=2), ALU.add)
                dve.drain()
                for s in range(TILES):
                    dve.bn_stats(fin_stats[0:SUB, s, :], out_c[0:SUB, s, :])
                dve.drain()
                for s in range(TILES):
                    dve.bn_aggr(fin_mv[0:SUB, s, :], fin_stats[0:SUB, s, :])
                dve.drain().then_inc(f_mv, 1)
                dve.wait_ge(f_std, c + 1)
                dve.reciprocal(fin_r[0:SUB, :], fin_s[0:SUB, :])
                dve.drain()
                dve.scalar_tensor_tensor(fin_m[0:SUB, :], fin_mv[0:SUB, :, 0], -1.0, fin_r[0:SUB, :],
                                         ALU.mult, ALU.mult)
                dve.drain().then_inc(f_r, 1)
            return finish_nodes

        def pass_matmuls(pe, L, layer, fast=False):
            finish_nodes = finish_nodes_pe(pe) if layer == 1 else mlp_pe(pe, L.group_done)
            width = D if layer == 0 else ROW
            msgs = PAIRS if layer == 0 else 2

            def edge_products(i, u, g, pairs):
                for q in pairs:
                    if q == 0:
                        pe.wait_ge(L.edge_in[u], 16 * i + 16)
                    if not (first_round(i) and g == 0):
                        pe.wait_ge(L.summed, PAIRS * (g - 1) + q + 1)
                    for h in range(2):
                        j = 2 * q + h
                        out = banks[q][:, h * D:(h + 1) * D]
                        last = pe.matmul(out, edge_in[:, u, j * P:(j + 1) * P], w_edge[:, :], start=True, stop=True)
                    last.then_inc(L.edge_done, 1)

            def spread_ed(i, u, g):
                pe.wait_ge(L.spread_hot, g + 1)
                pe.wait_ge(L.ed_in[u % RING], 16 * (i + u // RING) + 16)
                for j in range(J):
                    last = pe.matmul(banks[u % 2][:, j * PARTS * HEADS:(j + 1) * PARTS * HEADS],
                                     hot_t[:, j * P:(j + 1) * P], ed_win[:, u % RING, :], start=True, stop=True)
                last.then_inc(L.edge_done, 1)

            def sum_window(hot, u, dst_sem):
                for j in range(J):
                    last = pe.matmul(agg_ps[0:WIN, 0:width], onehot[:, hot, j, :], rows[:, u, j, 0:width],
                                     start=(j == 0), stop=(j == J - 1))
                last.then_inc(dst_sem, 1)

            def sum_first(u, g):
                pe.wait_ge(L.onehot_ready, g + 1)
                pe.wait_ge(L.msg_ready, msgs * (g + 1))
                sum_window(u % 2, u, L.agg_ready)

            def turn_first(g, at_start):
                pe.wait_ge(L.agg_copied, g + 1)
                if not at_start:
                    pe.wait_ge(L.group_done, g)
                turn(pe, L, L.turned)

            def extras(u, g):
                windows = pe.value_load(plan[0:1, 1, bass.ds(g, 1)], min_val=1, max_val=CHUNKS * 8)
                before = pe.value_load(plan[0:1, 2, bass.ds(g, 1)], min_val=0, max_val=1 << 20)
                with pe.If(windows > 1):
                    with pe.Fori(1, windows) as k:
                        pe.wait_ge(L.x_onehot, before + k)
                        sum_window(2, u, L.x_agg)
                        pe.wait_ge(L.x_copied, before + k)
                        turn(pe, L, L.x_turned)

            def body(i, u, g):
                n = g if first_round(i) else RING
                if layer == 0:
                    edge_products(i, u, g, range(PAIRS - 1))
                if n >= 2 and not fast:
                    extras((u - 2) % RING, g - 2)
                if n >= 1:
                    sum_first((u - 1) % RING, g - 1)
                if layer == 0:
                    edge_products(i, u, g, range(PAIRS - 1, PAIRS))
                if n >= 1:
                    turn_first(g - 1, n == 1)
                if fast and layer == 1:
                    spread_ed(i, u + 1, g + 1)
            if fast and layer == 1:
                spread_ed(0, 0, 0)
            c0 = rounds(pe, body, finish_nodes if fast else None)
            if not fast:
                extras(RING - 2, GROUPS - 2)
            sum_first(RING - 1, GROUPS - 1)
            turn_first(GROUPS - 1, False)
            if not fast:
                extras(RING - 1, GROUPS - 1)
            last_nodes(pe, finish_nodes, c0 if fast else 0)

        def pass_act(act, L, layer, fast=False):
            width = D if layer == 0 else ROW

            def copy_window(dst_sem):
                act.copy(agg_sb[:, 0:width], agg_ps[0:WIN, 0:width]).then_inc(dst_sem, 1)

            def copy_first(g, at_start):
                act.wait_ge(L.agg_ready, g + 1)
                if not at_start:
                    act.wait_ge(L.group_done, g)
                copy_window(L.agg_copied)

            def extras(g):
                windows = act.value_load(plan[0:1, 1, bass.ds(g, 1)], min_val=1, max_val=CHUNKS * 8)
                before = act.value_load(plan[0:1, 2, bass.ds(g, 1)], min_val=0, max_val=1 << 20)
                with act.If(windows > 1):
                    with act.Fori(1, windows) as k:
                        act.wait_ge(L.x_agg, before + k)
                        copy_window(L.x_copied)

            def body(i, u, g):
                start = first_round(i) and g == 0
                if layer == 0:
                    for q in range(PAIRS):
                        if q == 1 and not start:
                            copy_first(g - 1, first_round(i) and g == 1)
                        act.wait_ge(L.summed, PAIRS * g + q + 1)
                        pair = rows[:, u, 2 * q:2 * q + 2, 0:D]
                        act.activation(pair, pair, ACT.Relu).then_inc(L.msg_ready, 1)
                else:
                    if fast:
                        act.wait_ge(L.scored, g + 1)
                    else:
                        act.wait_ge(L.edge_in[u], 16 * i + 16)
                        act.wait_ge(L.rows_in[u], 16 * J * (i + 1))
                    act.activation(rows[:, u, :, D:ROW], expo[:, u, :].rearrange("p (j h) -> p j h", j=J),
                                   ACT.Exp).then_inc(L.summed, 1)
                    if not start:
                        copy_first(g - 1, first_round(i) and g == 1)
                if not start and not fast:
                    extras(g - 1)
            finish_nodes = finish_nodes_act(act, L.group_done) if layer == 1 else mlp_act(act)
            c0 = rounds(act, body, finish_nodes if fast else None)
            copy_first(GROUPS - 1, False)
            if not fast:
                extras(GROUPS - 1)
            last_nodes(act, finish_nodes, c0 if fast else 0)

        def pass_vector(dve, L, layer, fast=False):
            window_base = dve.alloc_register(f"window_base{layer}{fast}")

            def score_edges(i, u, g):
                js = lambda ap: ap.rearrange("p (j h) -> p j h", j=J)
                parts = banks[u % 2][:, 0:J * PARTS * HEADS].rearrange("p (j q h) -> p j h q", j=J, q=PARTS)
                dve.wait_ge(L.edge_done, g + 1)
                dve.tensor_reduce(js(score[:, 2, :]), parts, AX.X, ALU.add)
                dve.drain()
                dve.wait_ge(L.rows_in[u], 16 * J * (i + 1))
                dve.tensor_tensor(js(score[:, 0, :]), js(score[:, 2, :]), rows[:, u, :, D:ROW], ALU.add)
                dve.tensor_scalar(score[:, 1, :], score[:, 2, :], es_top[:, 0:1], None, ALU.add)
                dve.drain()
                dve.scalar_tensor_tensor(lrelu[:, :, :], score[:, 0:2, :], SLOPE, score[:, 0:2, :], ALU.mult, ALU.max)
                dve.drain()
                dve.tensor_scalar(score[:, 2, :], lrelu[:, 0, :], 0.0, NEG_NEAR, ALU.is_equal, ALU.mult)
                dve.tensor_tensor(score[:, 0, :], lrelu[:, 0, :], lrelu[:, 1, :], ALU.subtract)
                dve.drain()
                dve.tensor_tensor(expo[:, u, :], score[:, 0, :], score[:, 2, :], ALU.add).then_inc(L.scored, 1)

            def add_window(base):
                at = bass.ds(base, WIN)
                last = dve.tensor_tensor(acc[:, :, at], acc[:, :, at],
                                         turn_ps[:, 0:HALF * WIN].rearrange("p (k n) -> p k n", k=HALF), ALU.add)
                if layer == 1:
                    last = dve.tensor_tensor(den[:, at], den[:, at],
                                             turn_ps[0:HEADS, HALF * WIN:(HALF + 1) * WIN], ALU.add)
                return last

            def make_hot_t(i, u, g):
                dve.wait_ge(L.dst_in[u % 2], 32 * i + 16 * (u // 2) + 16)
                if not (isinstance(g, int) and g == 0):
                    dve.wait_ge(L.edge_done, g)
                dve.tensor_scalar(hot_t[:, :], dst_t[:, u % 2, :], node_at[:, bass.ds(g, 1)], None,
                                  ALU.is_equal).then_inc(L.spread_hot, 1)

            def finish(u, g):
                base = dve.value_load(plan[0:1, 0, bass.ds(g, 1)], min_val=0, max_val=NODES)
                if fast:
                    dve.wait_ge(L.turned, g + 1)
                    add_window(base)
                    dve.drain().then_inc(L.group_done, 1)
                    return
                windows = dve.value_load(plan[0:1, 1, bass.ds(g, 1)], min_val=1, max_val=CHUNKS * 8)
                before = dve.value_load(plan[0:1, 2, bass.ds(g, 1)], min_val=0, max_val=1 << 20)
                dve.wait_ge(L.turned, g + 1)
                add_window(base)
                with dve.If(windows > 1):
                    dve.tensor_copy(off_here[:, :], offsets(g))
                    with dve.Fori(1, windows) as k:
                        dve.drain()
                        dve.tensor_scalar(off_here[:, :], off_here[:, :], float(WIN), None, ALU.subtract)
                        dve.drain()
                        make_onehot(2, off_here[:, :], L.x_onehot)
                        dve.wait_ge(L.x_turned, before + k)
                        dve.reg_mov(window_base, base + k * WIN)
                        add_window(dve.snap(window_base, min_val=0, max_val=NODES))
                dve.drain().then_inc(L.group_done, 1)

            def offsets(g):
                return dst_off[:, bass.ds(g, 1), :].rearrange("p g j -> p (g j)")

            def make_onehot(hot, off, dst_sem):
                dve.tensor_tensor(onehot[:, hot, :, :], off.unsqueeze(2).to_broadcast([P, J, WIN]),
                                  iota[:, :].unsqueeze(1).to_broadcast([P, J, WIN]), ALU.is_equal).then_inc(dst_sem, 1)

            def body(i, u, g):
                make_onehot(u % 2, offsets(g), L.onehot_ready)
                if layer == 0:
                    dve.wait_ge(L.rows_in[u], 16 * J * (i + 1))

                    def add_bias(q):
                        pair = rows[:, u, 2 * q:2 * q + 2, 0:D]
                        dve.tensor_tensor(pair, pair, b_edge[:, :].unsqueeze(1).to_broadcast([P, 2, D]), ALU.add)

                    def add_edges(q):
                        dve.wait_ge(L.edge_done, PAIRS * g + q + 1)
                        pair = rows[:, u, 2 * q:2 * q + 2, 0:D]
                        dve.tensor_tensor(pair, pair, banks[q][:, :].rearrange("p (j d) -> p j d", j=2),
                                          ALU.add).then_inc(L.summed, 1)

                    add_bias(0)
                    add_bias(1)
                    dve.drain()
                    add_edges(0)
                    add_bias(2)
                    add_edges(1)
                    add_bias(3)
                    dve.drain()
                    add_edges(2)
                    add_edges(3)
                else:
                    if fast:
                        score_edges(i, u, g)
                    dve.wait_ge(L.summed, g + 1)
                    for q in range(2):
                        js = slice(q * J // 2, (q + 1) * J // 2)
                        z = rows[:, u, js, 0:D].rearrange("p j (h f) -> p j h f", h=HEADS)
                        w = rows[:, u, js, D:ROW].unsqueeze(3).to_broadcast([P, J // 2, HEADS, HEAD_D])
                        dve.tensor_tensor(z, z, w, ALU.mult).then_inc(L.msg_ready, 1)
                if fast and layer == 1:
                    make_hot_t(i, u + 1, g + 1)
                if not (first_round(i) and g == 0):
                    finish((u - 1) % RING, g - 1)
            if fast and layer == 1:
                make_hot_t(0, 0, 0)
            finish_nodes = finish_nodes_dve(dve) if layer == 1 else mlp_dve(dve, int(fast))
            c0 = rounds(dve, body, finish_nodes if fast else None)
            finish(RING - 1, GROUPS - 1)
            last_nodes(dve, finish_nodes, c0 if fast else 0)


        def nodes(i, b):
            return bass.ds((2 * i + b) * CHUNK, CHUNK)

        def tiles(i, b):
            return bass.ds((2 * i + b) * TILES, TILES)

        def steps(eng, body, peel=1):
            with eng.Fori(0, STEPS - peel) as i:
                body(i)
            for i in range(STEPS - peel, STEPS):
                body(i)

        def ahead(stage, i, b, n):
            if not (isinstance(i, int) and 2 * i + b + n >= CHUNKS):
                stage(i + (b + n) // 2, (b + n) % 2)

        def is_last(i):
            return isinstance(i, int) and i == STEPS - 1

        @block.sync
        def _(sp):
            for u in range(RING):
                sp.dma_start(idx[:, u, :], t["src_idx"][u]).then_inc(layer0.idx_in[u], 16)
            for out, of in ((b_edge[:, :], t["b_edge"].to_broadcast([P, D])), (w_edge[:, :], t["w_edge"]),
                            (eps1[:, :], t["eps"].to_broadcast([P, 1]))):
                sp.dma_start(out, of).then_inc(edge_w_in, 16)
            for out, of in ((firsts[:, 0, :], t["first"].to_broadcast([P, GROUPS])),
                            (firsts[:, 1, :], t["last"].to_broadcast([P, GROUPS])),
                            (dst_raw[:, :], t["dst_pm"])):
                sp.dma_start(out, of).then_inc(dst_in, 16)
            for u in range(RING):
                sp.dma_start(edge_in[:, u, :], t["edge_t"][u]).then_inc(layer0.edge_in[u], 16)
            for out, of in ((cols[:, 0, :], t["b1"]), (cols[:, 1, :], t["b2"]),
                            (cols[:, 2, :], t["gamma"]), (cols[:, 3, :], t["beta"]),
                            (w1[:, :, :], t["w1"]), (w2[:, :, :], t["w2"]), (wz[:, :, 0:D], t["wz"]),
                            (att[:, 0, :], t["att_src"].to_broadcast([P, D])),
                            (att[:, 1, :], t["att_dst"].to_broadcast([P, D])),):
                sp.dma_start(out, of).then_inc(const_in, 16)
            sp.wait_ge(ends_ready, 1)
            one_window = sp.value_load(single[0:1, 0:1], min_val=0, max_val=1)
            with sp.If(one_window > 0):
                pass_loads(sp, layer0, 0, fast=True)
            with sp.Else():
                pass_loads(sp, layer0, 0)

            sp.wait_ge(acc_zeroed, 1)
            sp.dma_start(ed_parts[NPAD:NPAD + WIN, :], zero_b[:, :]).then_inc(l_tail, 16)
            sp.wait_ge(a_pe2, CHUNKS)

            def load_b(i, b):
                sp.wait_ge(l_res[b], i)
                sp.sem_inc(passed, 1)
                sp.dma_start(x_in[b], t["x_t"][:, :, nodes(i, b)]).then_inc(l_in[b], 16)

            def table_rows(tab, i, b):
                return tab[nodes(i, b), :].rearrange("(s p) c -> p s c", s=TILES)

            def move_b(i):
                for b in range(2):
                    ahead(load_b, i, b, 4)
                    sp.wait_ge(l_zc[b], i + 1)
                    sp.sem_inc(passed, 1)
                    sp.dma_start(table_rows(z_tab, i, b), z_sb[b][0:SUB]).then_inc(l_zout[b], 16)
                    sp.wait_ge(l_split, 2 * i + b + 1)
                    sp.sem_inc(passed, 1)
                    sp.dma_start(table_rows(ed_parts, i, b),
                                 ed_split[0:SUB, tiles(i, b)].rearrange("p s q h -> p s (q h)")).then_inc(l_eout[b], 16)
            for c in range(4):
                load_b(c // 2, c % 2)
            steps(sp, move_b, peel=2)
            for b in range(2):
                sp.wait_ge(l_zout[b], 16 * STEPS)
                sp.wait_ge(l_eout[b], 16 * STEPS)
            sp.wait_ge(l_tail, 16)
            sp.wait_ge(mode_ready, 1)
            bounded = sp.value_load(mode[0:1, 0:1], min_val=0, max_val=1)
            with sp.If(bounded > 0):
                pass_loads(sp, layer1, 1, fast=True)
            with sp.Else():
                for tab, lo in ((es_tab, 0), (ed_tab, HEADS)):
                    sp.dma_start(tab.rearrange("(s p) c -> p s c", p=SUB),
                                 score_all[0:SUB, :, lo:lo + HEADS]).then_inc(tabs_out, 16)
                sp.wait_ge(tabs_out, 32)
                with sp.Fori(0, GROUPS // 2) as i:
                    for u in range(2):
                        g = i * 2 + u
                        sp.wait_ge(s_rows[u], 2 * 16 * J * i)
                        sp.dma_start(idx[:, u, :], t["src_idx"][g]).then_inc(s_idx[u], 16)
                        sp.dma_start(idx[:, 2 + u, :], t["dst_idx"][g]).then_inc(s_idx[u], 16)
                    for u in range(2):
                        g = i * 2 + u
                        sp.wait_ge(s_score, g + 1)
                        sp.dma_start(score_tab[g], expo[:, u, :]).then_inc(s_stored[u], 16)
                for u in range(2):
                    sp.wait_ge(s_stored[u], 16 * (GROUPS // 2))
                line = score_tab.rearrange("g p c -> (g p c)").rearrange("(q n) -> q n", q=P)
                sp.dma_start(acc_line(0), line).then_inc(m_in, 16)
                for n in range(3):
                    sp.dma_start(line_dst(n), t["dst_ext"][:, n:n + EPAD].rearrange("a (q n) -> (a q) n", q=P)).then_inc(m_in, 16)
                sp.wait_ge(m_done, 1)
                oline = expo_tab.rearrange("g p c -> (g p c)").rearrange("(q n) -> q n", q=P)
                sp.dma_start(oline, acc_line(0)).then_inc(m_out, 16)
                sp.wait_ge(m_out, 16)
                pass_loads(sp, layer1, 1)

        @block.gpsimd
        def _(pool):
            nc.gpsimd.iota(iota_i[:, :], pattern=[[1, WIN]], base=0, channel_multiplier=0).then_inc(consts, 1)
            nc.gpsimd.memset(ident[:, :], 0.0)
            pool.drain()
            nc.gpsimd.affine_select(out=ident[:, :], in_=ident[:, :], compare_op=ALU.not_equal, fill=1.0, base=0,
                                    pattern=[[-1, P]], channel_multiplier=1)
            nc.gpsimd.iota(part_i[:, :], pattern=[[0, 1]], base=0, channel_multiplier=1)
            pool.drain().then_inc(consts, 1)
            pass_gathers(pool, layer0, 0)

            pool.wait_ge(a_pe1, HALF * CHUNKS)
            pool.sem_inc(passed, 1)
            nc.gpsimd.memset(acc[:, :, :], 0.0)

            def keep_b(i):
                for b in range(2):
                    pool.wait_ge(l_x[b], i + 1)
                    pool.sem_inc(passed, 1)
                    nc.gpsimd.tensor_copy(node_x[:, :, nodes(i, b)], buf_n[b]).then_inc(l_keep[b], 1)
                    pool.wait_ge(l_zc[b], i + 1)
                    pool.sem_inc(passed, 1)
                    rest = [score_all[0:SUB, tiles(i, b), HEADS:], ed_rest[0:SUB, 0], ed_rest[0:SUB, 1]]
                    for q in range(PARTS):
                        part_q = ed_split[0:SUB, tiles(i, b), q, :]
                        nc.gpsimd.tensor_copy(part_q, rest[q])
                        pool.drain()
                        if q < PARTS - 1:
                            nc.gpsimd.tensor_tensor(rest[q + 1], rest[q], part_q, ALU.subtract)
                            pool.drain()
                    pool.sem_inc(l_split, 1)
            steps(pool, keep_b)
            pool.drain().then_inc(layer1.acc_zero, 1)
            for b in range(2):
                pool.wait_ge(l_zout[b], 16 * STEPS)
                pool.wait_ge(l_eout[b], 16 * STEPS)
            pool.wait_ge(l_tail, 16)
            pool.wait_ge(mode_ready, 1)
            bounded = pool.value_load(mode[0:1, 0:1], min_val=0, max_val=1)
            with pool.If(bounded > 0):
                pass_gathers(pool, layer1, 1)
            with pool.Else():
                with pool.Fori(0, GROUPS // 2) as i:
                    for u in range(2):
                        g = i * 2 + u
                        pool.wait_ge(s_idx[u], 32 * i + 32)
                        pool.sem_inc(passed, 1)
                        for j in range(J):
                            for n, tab in ((u, es_tab), (2 + u, ed_tab)):
                                nc.gpsimd.indirect_dma_start(
                                    score_rows(n)[:, j * HEADS:(j + 1) * HEADS], None, tab,
                                    bass.IndirectOffsetOnAxis(ap=idx[:, n, j:j + 1], axis=0)).then_inc(s_rows[u], 16)
                pool.wait_ge(m_out, 16)
                nc.gpsimd.memset(acc[:, :, :], 0.0)
                nc.gpsimd.memset(den, 0.0)
                pool.drain().then_inc(layer1.acc_zero, 1)
                pass_gathers(pool, layer1, 1)

        @block.tensor
        def _(pe):
            pe.wait_ge(edge_w_in, 48)
            pe.wait_ge(consts, 2)
            pe.wait_ge(planned, 1)
            pe.transpose(banks[7][0:1, 0:CHUNKS], counts[0:CHUNKS, :], ident[0:CHUNKS, 0:CHUNKS]).then_inc(counted, 1)
            pe.wait_ge(ends_ready, 1)
            one_window = pe.value_load(single[0:1, 0:1], min_val=0, max_val=1)
            with pe.If(one_window > 0):
                pass_matmuls(pe, layer0, 0, fast=True)
            with pe.Else():
                pass_matmuls(pe, layer0, 0)
            pe.wait_ge(a_act2, CHUNKS)

            def mean_over(x, out, done):
                for k in range(HALF):
                    last = pe.matmul(banks[out][:, 0:CHUNK], mean_w[:, :], x[:, k, :], start=(k == 0), stop=(k == 1))
                last.then_inc(done, 1)

            def mean(i, b):
                pe.wait_ge(l_res[b], i + 1)
                mean_over(buf_r[b], b, l_mean)

            def variance(i, b):
                pe.wait_ge(l_sq, 2 * i + b + 1)
                mean_over(buf_r[b], 6 + b, l_var[b])

            def norm_and_project(i):
                for b in range(2):
                    ahead(variance, i, b, 1)
                    ahead(mean, i, b, 2)
                    pe.wait_ge(l_x[b], i + 1)
                    pe.wait_ge(l_zc[1 - b], i + b)
                    for s in range(TILES):
                        for k in range(HALF):
                            z = pe.matmul(psum[0:SUB, 2 + s, 0:D + 2 * HEADS], buf_n[b][:, k, s * SUB:(s + 1) * SUB],
                                          wz[:, k, :], start=(k == 0), stop=(k == 1))
                    z.then_inc(l_z[b], 1)
            mean(0, 0)
            variance(0, 0)
            mean(0, 1)
            pe.wait_ge(wz_ready, 1)
            steps(pe, norm_and_project, peel=2)

            pe.wait_ge(top_ready, 1)
            pe.transpose(banks[6][0:1, 0:SUB], es_max[0:SUB, :], ident[0:SUB, 0:SUB]).then_inc(top_turned, 1)
            pe.wait_ge(top_one, 1)
            pe.matmul(banks[7][:, 0:1], ones_row[:, :], choice[:, 0:1], start=True, stop=True).then_inc(top_all, 1)
            pe.wait_ge(mode_ready, 1)
            bounded = pe.value_load(mode[0:1, 0:1], min_val=0, max_val=1)
            with pe.If(bounded > 0):
                pe.wait_ge(layer1.acc_zero, 1)
                pass_matmuls(pe, layer1, 1, fast=True)
            with pe.Else():
                for n in range(2):
                    pe.wait_ge(m_last, n + 1)
                    pe.transpose(banks[0][0:HEADS, 0:P], lasts[:, 0:HEADS], ident[:, :])
                    pe.transpose(banks[0][0:HEADS, P:2 * P], lasts[:, HEADS:2 * HEADS], ident[:, :]).then_inc(m_lastT, 1)
                    pe.wait_ge(m_carry, n + 1)
                    pe.transpose(banks[1][:, 0:HEADS], carry_t[0:HEADS, n:n + P], ident[0:HEADS, 0:HEADS]).then_inc(m_carryT, 1)
                pe.wait_ge(layer1.acc_zero, 2)
                pass_matmuls(pe, layer1, 1)
        @block.scalar
        def _(act):
            act.wait_ge(zero_ready, 1)
            act.copy(acc[:, 1, :], zero_f[:, :].to_broadcast([P, ACC_W])).then_inc(acc_zeroed, 1)
            act.wait_ge(ends_ready, 1)
            one_window = act.value_load(single[0:1, 0:1], min_val=0, max_val=1)
            with act.If(one_window > 0):
                pass_act(act, layer0, 0, fast=True)
            with act.Else():
                pass_act(act, layer0, 0)
            act.wait_ge(bn_var, 1)
            act.activation(bn_tmp[:, :], mv[:, :, 1], ACT.Sqrt, bias=bn_eps[:, :]).then_inc(bn_sqrt, 1)
            act.wait_ge(bn_ready, 1)

            def batch_norm(i, b):
                act.wait_ge(l_var[b], i)
                for k in range(HALF):
                    ins = act.activation(buf_r[b][:, k, :], node_x[:, k, nodes(i, b)], ACT.Relu,
                                         bias=bn_shift[:, k:k + 1], scale=bn_scale[:, k:k + 1])
                ins.then_inc(l_bn, 1)

            def square(i, b):
                act.wait_ge(l_cen, 2 * i + b + 1)
                act.activation(buf_r[b], buf_c[b], ACT.Square).then_inc(l_sq, 1)

            def deviation(i, b):
                act.wait_ge(l_var[b], i + 1)
                act.wait_ge(l_x[b], i)
                act.activation(rstd[b], banks[6 + b][:, 0:CHUNK], ACT.Sqrt, bias=ln_eps[:, :]).then_inc(l_std, 1)

            def norm_and_project(i):
                for b in range(2):
                    ahead(deviation, i, b, 1)
                    ahead(batch_norm, i, b, 3)
                    ahead(square, i, b, 2)
                    act.wait_ge(l_z[b], i + 1)
                    act.wait_ge(l_zout[b], 16 * i)
                    act.copy(score_all[0:SUB, tiles(i, b), :], psum[0:SUB, 2:2 + TILES, D:D + 2 * HEADS])
                    act.copy(z_sb[b][0:SUB], psum[0:SUB, 2:2 + TILES, 0:ROW])
                    act.drain().then_inc(l_zc[b], 1)
            batch_norm(0, 0)
            batch_norm(0, 1)
            square(0, 0)
            deviation(0, 0)
            batch_norm(1, 0)
            square(0, 1)
            steps(act, norm_and_project, peel=2)
            act.wait_ge(mode_ready, 1)
            bounded = act.value_load(mode[0:1, 0:1], min_val=0, max_val=1)
            with act.If(bounded > 0):
                pass_act(act, layer1, 1, fast=True)
            with act.Else():
                pass_act(act, layer1, 1)
            act.wait_ge(f_out, 16 * (CHUNKS + (TAIL % SUB > 0)))

        @block.vector
        def _(dve):
            def step(ins=None):
                dve.drain()

            dve.wait_ge(consts, 2)
            dve.tensor_copy(part[:, :], part_i[:, :])
            dve.memset(zero_f[:, :], 0.0)
            dve.drain().then_inc(zero_ready, 1)
            dve.memset(zero_b[:, :], 0.0)
            dve.memset(ones_row[:, :], 1.0)
            dve.tensor_copy(iota[:, :], iota_i[:, :])
            dve.memset(mean_w[:, :], 1.0 / D)
            dve.memset(ln_eps[:, :], LN_EPS)
            dve.memset(bn_eps[:, :], BN_EPS)
            dve.wait_ge(dst_in, 48)
            dve.tensor_copy(first_f[:, :], firsts[:, 0, :])
            dve.tensor_copy(plan[:, 0, :], firsts[0:1, 0, :])
            step()
            dve.memset(node_at[:, GROUPS:], 0.0)
            dve.tensor_scalar(node_at[:, 0:GROUPS], first_f[:, :], part[:, 0:1], None, ALU.add)
            dve.tensor_tensor(plan[:, 1, :], firsts[0:1, 1, :], firsts[0:1, 0, :], ALU.subtract)
            step()
            dve.tensor_scalar(plan[:, 1, :], plan[:, 1, :], WIN.bit_length() - 1, None, ALU.arith_shift_right)
            step()
            dve.tensor_copy(plan_f[:, 0, :], plan[:, 1, :])
            dve.memset(plan_f[:, 1, :], 1.0)
            step()
            dve.tensor_tensor_scan(plan_f[:, 2, :], plan_f[:, 1, :], plan_f[:, 0, :], 0.0, ALU.mult, ALU.add)
            dve.tensor_scalar(plan[:, 1, :], plan_f[:, 0, :], 1.0, None, ALU.add)
            step()
            dve.tensor_tensor(plan[:, 2, :], plan_f[:, 2, :], plan_f[:, 0, :], ALU.subtract)
            dve.tensor_scalar(counts[:, :], part[:, :], float(CHUNK), float(CHUNK), ALU.mult, ALU.add)
            step()
            dve.tensor_scalar(is_before, first_f[:, :], counts[:, 0:1], None, ALU.is_lt)
            step()
            dve.tensor_reduce(counts[:, :], is_before, AX.X, ALU.add)
            dve.drain().then_inc(planned, 1)
            dve.tensor_tensor(dst_off[:, :, :], dst_raw[:, :].rearrange("p (g j) -> p g j", j=J),
                              first_f[:, :].unsqueeze(2).to_broadcast([P, GROUPS, J]), ALU.subtract)
            dve.wait_ge(counted, 1)
            dve.tensor_copy(node_ends[:, 1:CHUNKS + 1], banks[7][0:1, 0:CHUNKS])
            dve.tensor_scalar(is_early[:, 0:CHUNKS], banks[7][0:1, 0:CHUNKS], float(GROUPS), None, ALU.is_lt)
            dve.memset(node_ends[:, 0:1], 0)
            dve.tensor_reduce(choice[:, 1:2], plan[:, 1, :], AX.X, ALU.max)
            step()
            dve.tensor_scalar(node_ends[:, 1:CHUNKS + 1], node_ends[:, 1:CHUNKS + 1], RING.bit_length() - 1, None,
                              ALU.arith_shift_right)
            dve.tensor_reduce(is_early[:, CHUNKS:CHUNKS + 1], is_early[:, 0:CHUNKS], AX.X, ALU.add)
            dve.tensor_scalar(single[:, :], choice[:, 1:2], 1.0, None, ALU.is_le)
            step()
            dve.tensor_copy(node_ends[:, CHUNKS + 1:CHUNKS + 2], is_early[:, CHUNKS:CHUNKS + 1])
            dve.drain().then_inc(ends_ready, 1)
            dve.memset(acc[:, 0, :], 0.0)
            dve.wait_ge(edge_w_in, 48)
            dve.tensor_scalar(eps1[:, :], eps1[:, :], 1.0, None, ALU.add)
            dve.wait_ge(acc_zeroed, 1)
            dve.wait_ge(const_in, 16 * WEIGHT_LOADS)
            dve.sem_inc(passed, 1)
            step()
            dve.tensor_scalar(w1x[:, :, :], w1, eps1[:, 0:1], None, ALU.mult).then_inc(w1x_ready, 1)
            one_window = dve.value_load(single[0:1, 0:1], min_val=0, max_val=1)
            with dve.If(one_window > 0):
                pass_vector(dve, layer0, 0, fast=True)
            with dve.Else():
                pass_vector(dve, layer0, 0)
            step()
            for k in range(HALF):
                dve.bn_aggr(mv[:, k, :], stats[:, k, :, :].rearrange("p c s -> p (c s)"))
            dve.drain().then_inc(bn_var, 1)
            dve.wait_ge(bn_sqrt, 1)
            dve.reciprocal(bn_shift[:, :], bn_tmp[:, :])
            step()
            dve.tensor_tensor(bn_scale[:, :], bn_shift[:, :], cols[:, 2, :], ALU.mult)
            step()
            dve.tensor_tensor(bn_tmp[:, :], bn_scale[:, :], mv[:, :, 0], ALU.mult)
            step()
            dve.tensor_tensor(bn_shift[:, :], cols[:, 3, :], bn_tmp[:, :], ALU.subtract)
            dve.drain().then_inc(bn_ready, 1)

            def residual(i, b):
                dve.wait_ge(l_in[b], 16 * i + 16)
                dve.wait_ge(l_bn, 2 * i + b + 1)
                dve.tensor_tensor(buf_r[b], x_in[b], buf_r[b], ALU.add).then_inc(l_res[b], 1)

            def centre(i, b):
                dve.wait_ge(l_x[b], i)
                dve.wait_ge(l_mean, 2 * i + b + 1)
                dve.tensor_tensor(buf_c[b], buf_r[b], banks[b][:, 0:CHUNK].unsqueeze(1).to_broadcast([P, HALF, CHUNK]),
                                  ALU.subtract).then_inc(l_cen, 1)

            def scale(i, b):
                dve.wait_ge(l_std, 2 * i + b + 1)
                dve.reciprocal(rstd[b], rstd[b])
                step()
                dve.wait_ge(l_z[b], i)
                dve.wait_ge(l_keep[b], i)
                dve.tensor_tensor(buf_n[b], buf_c[b], rstd[b].unsqueeze(1).to_broadcast([P, HALF, CHUNK]),
                                  ALU.mult).then_inc(l_x[b], 1)

            def norm(i):
                for b in range(2):
                    ahead(centre, i, b, 2)
                    ahead(residual, i, b, 3)
                    ahead(scale, i, b, 1)
            residual(0, 0)
            residual(0, 1)
            ends_k = [(n, k) for n in range(2) for k in range(HALF)]
            for m, (n, k) in enumerate(ends_k):
                dve.tensor_tensor(wz_tmp[:, m, :], wz[:, k, 0:D], att[:, n, :], ALU.mult)
            step()
            for m, (n, k) in enumerate(ends_k):
                dve.tensor_reduce(wz[:, k, D + n * HEADS:D + (n + 1) * HEADS],
                                  wz_tmp[:, m, :].rearrange("p (h f) -> p h f", h=HEADS), AX.X, ALU.add)
            dve.drain().then_inc(wz_ready, 1)
            centre(0, 0)
            centre(0, 1)
            residual(1, 0)
            scale(0, 0)
            steps(dve, norm, peel=2)

            for b in range(2):
                dve.wait_ge(l_zc[b], STEPS)
            es = score_all[0:SUB, :, 0:HEADS]
            dve.scalar_tensor_tensor(es_abs[0:SUB], es, -1.0, es, ALU.mult, ALU.max)
            step()
            dve.tensor_reduce(es_max[0:SUB, :], es_abs[0:SUB].rearrange("p s h -> p (s h)"), AX.X,
                              ALU.max).then_inc(top_ready, 1)
            dve.wait_ge(top_turned, 1)
            dve.tensor_reduce(choice[:, 0:1], banks[6][0:1, 0:SUB], AX.X, ALU.max)
            dve.tensor_reduce(choice[:, 1:2], plan[:, 1, :], AX.X, ALU.max)
            dve.drain().then_inc(top_one, 1)
            dve.wait_ge(top_all, 1)
            dve.tensor_copy(es_top[:, :], banks[7][:, 0:1])
            dve.tensor_scalar(choice[:, 2:3], choice[:, 0:1], ES_LIMIT, None, ALU.is_le)
            dve.tensor_scalar(choice[:, 3:4], choice[:, 1:2], 1.0, None, ALU.is_le)
            step()
            dve.tensor_tensor(mode[:, :], choice[:, 2:3], choice[:, 3:4], ALU.mult)
            dve.drain().then_inc(mode_ready, 1)

            bounded = dve.value_load(mode[0:1, 0:1], min_val=0, max_val=1)
            with dve.If(bounded > 0):
                dve.wait_ge(layer1.acc_zero, 1)
                for b in range(2):
                    dve.wait_ge(l_zout[b], 16 * STEPS)
                    dve.wait_ge(l_eout[b], 16 * STEPS)
                dve.memset(den, 0.0)
                dve.drain()
                pass_vector(dve, layer1, 1, fast=True)
            with dve.Else():
                with dve.Fori(0, GROUPS // 2) as i:
                    for u in range(2):
                        g = i * 2 + u
                        a, b = score_rows(u), score_rows(2 + u)
                        e = expo[:, u, :]
                        dve.wait_ge(s_stored[u], 16 * i)
                        dve.wait_ge(s_rows[u], 2 * 16 * J * (i + 1))
                        dve.tensor_tensor(a, a, b, ALU.add)
                        step()
                        dve.scalar_tensor_tensor(b, a, SLOPE, a, ALU.mult, ALU.max)
                        step()
                        dve.tensor_scalar(a, b, 0.0, NEG, ALU.is_equal, ALU.mult)
                        step()
                        dve.tensor_tensor(e, a, b, ALU.add).then_inc(s_score, 1)

                dve.wait_ge(m_in, 64)
                before, here, after = (line_dst(n) for n in range(3))
                dve.tensor_tensor(pen_in, here, before, ALU.not_equal)
                dve.tensor_tensor(pen_out, here, after, ALU.not_equal)
                step()
                dve.tensor_scalar(pen_in, pen_in, FAR, None, ALU.mult)
                dve.tensor_scalar(pen_out, pen_out, FAR, None, ALU.mult)
                dve.memset(carry_t[0:HEADS, :], FAR)
                step()
                e = acc_line(0).rearrange("p (n h) -> p n h", h=HEADS)
                f = acc_line(1).rearrange("p (n h) -> p n h", h=HEADS)
                for n in range(2):
                    pen, data, way = ((pen_in, e, slice(None)), (pen_out, f, slice(None, None, -1)))[n]
                    end = (LINE - 1, 0)[n]
                    for h in range(HEADS):
                        dve.tensor_tensor_scan(run_max[:, way], pen[:, way], data[:, way, h], FAR, ALU.add, ALU.max)
                        step()
                        dve.tensor_copy(lasts[:, h:h + 1], run_max[:, end:end + 1])
                        dve.tensor_reduce(lasts[:, HEADS + h:HEADS + h + 1], pen, AX.X, ALU.min)
                        step()
                    dve.drain().then_inc(m_last, 1)
                    dve.wait_ge(m_lastT, n + 1)
                    dve.tensor_copy(carry_sb[0:HEADS, :], banks[0][0:HEADS, 0:2 * P])
                    step()
                    dve.tensor_tensor_scan(carry_t[0:HEADS, 1:P + 1][:, way], carry_sb[0:HEADS, P:2 * P][:, way],
                                           carry_sb[0:HEADS, 0:P][:, way], FAR, ALU.add, ALU.max)
                    step()
                    if n == 1:
                        dve.tensor_copy(carry_sb[0:HEADS, 0:P], carry_t[0:HEADS, 1:P + 1])
                        step()
                        dve.memset(carry_t[0:HEADS, P:P + 1], FAR)
                        dve.tensor_copy(carry_t[0:HEADS, 1:P], carry_sb[0:HEADS, 1:P])
                        step()
                    dve.drain().then_inc(m_carry, 1)
                    dve.wait_ge(m_carryT, n + 1)
                    dve.tensor_copy(carry[:, 0:HEADS], banks[1][:, 0:HEADS])
                    step()
                    for h in range(HEADS):
                        out = f[:, :, h] if n == 0 else run_max
                        dve.tensor_tensor_scan(out[:, way], pen[:, way], data[:, way, h], carry[:, h:h + 1],
                                               ALU.add, ALU.max)
                        step()
                        if n == 1:
                            dve.tensor_tensor(e[:, :, h], e[:, :, h], run_max, ALU.subtract)
                            step()
                dve.tensor_scalar(acc_line(0), acc_line(0), FLOOR, None, ALU.max).then_inc(m_done, 1)
                dve.wait_ge(layer1.acc_zero, 2)
                pass_vector(dve, layer1, 1)


def kernel(x, src, dst, edge_attr_128, L0_gnn_W_edge, L0_gnn_b_edge, L0_gnn_W1, L0_gnn_b1, L0_gnn_W2, L0_gnn_b2,
           L0_gnn_eps, L0_gnn_gamma, L0_gnn_beta, L1_gnn_W, L1_gnn_att):
    import numpy as np
    import concourse.bacc as bacc
    from concourse.bass_utils import run_bass_kernel_spmd

    x, edge = np.asarray(x), np.asarray(edge_attr_128)
    pad = EPAD - EDGES
    src_p = np.concatenate([np.asarray(src), np.zeros(pad, np.int32)])
    dst_p = np.concatenate([np.asarray(dst), np.full(pad, NODES, np.int32)])
    edge_p = np.concatenate([edge, np.zeros((pad, EDGE_D), edge.dtype)])
    x_t = np.zeros((D, NPAD), x.dtype)
    x_t[:, :NODES] = x.T
    by_half = lambda w: np.ascontiguousarray(np.asarray(w).reshape(HALF, P, -1).transpose(1, 0, 2))
    by_col = lambda v: np.ascontiguousarray(np.asarray(v).reshape(HALF, P).T)
    att = np.asarray(L1_gnn_att)
    end = np.full(1, -1, np.int32)
    arrays = {
        "x": x,
        "src_idx": src_p.reshape(GROUPS, P, J),
        "dst_idx": dst_p.reshape(GROUPS, P, J),
        "dst_pm": dst_p.reshape(GROUPS, P, J).transpose(1, 0, 2).reshape(P, GROUPS * J),
        "dst_ext": np.concatenate([end, dst_p, end]).reshape(1, EPAD + 2),
        "dst_jp": np.concatenate([dst_p, np.full(GROUP, NODES, np.int32)]).reshape(GROUPS + 1, P, J)
                    .transpose(0, 2, 1).reshape(GROUPS + 1, 1, GROUP),
        "first": dst_p[::GROUP].reshape(1, GROUPS),
        "last": dst_p[GROUP - 1::GROUP].reshape(1, GROUPS),
        "edge_t": edge_p.reshape(GROUPS, P, J, EDGE_D).transpose(0, 3, 2, 1).reshape(GROUPS, EDGE_D, GROUP),
        "x_t": by_half(x_t),
        "w_edge": np.asarray(L0_gnn_W_edge),
        "b_edge": np.asarray(L0_gnn_b_edge).reshape(1, D),
        "w1": by_half(L0_gnn_W1), "w2": by_half(L0_gnn_W2),
        "b1": by_col(L0_gnn_b1), "b2": by_col(L0_gnn_b2),
        "gamma": by_col(L0_gnn_gamma), "beta": by_col(L0_gnn_beta),
        "eps": np.asarray(L0_gnn_eps).reshape(1, 1),
        "wz": by_half(np.asarray(L1_gnn_W).transpose(1, 0, 2).reshape(D, D)),
        "att_src": att[:, :HEAD_D].reshape(1, D), "att_dst": att[:, HEAD_D:].reshape(1, D),
    }
    nc = bacc.Bacc("TRN2", target_bir_lowering=False, num_devices=1)
    feeds, t = {}, {}
    for name, a in arrays.items():
        a = np.ascontiguousarray(a)
        feeds[f"in_{name}"] = a
        t[name] = nc.dram_tensor(f"in_{name}", a.shape, mybir.dt.from_np(a.dtype), kind="ExternalInput").ap()
    t["out"] = nc.dram_tensor("out_0", (NODES, D), F32, kind="ExternalOutput").ap()
    build(nc, t)
    r = run_bass_kernel_spmd(nc, [feeds], core_ids=[0])
    return r.results[0]["out_0"]
```
